# Optimizing a Trainium2 kernel written in Bass

```python
import numpy as np
import jax
import jax.numpy as jnp

def _softmax(x, axis=-1):
    return jax.nn.softmax(x, axis=axis)

def _gelu(x):
    return jax.nn.gelu(x, approximate=True)

def _silu(x):
    return jax.nn.silu(x)

def _sigmoid(x):
    return jax.nn.sigmoid(x)

def _layernorm(x, axis=-1, eps=1e-05):
    m = jnp.mean(x, axis=axis, keepdims=True)
    v = jnp.var(x, axis=axis, keepdims=True)
    return (x - m) / jnp.sqrt(v + eps)

def _scatter_add(tgt, idx, src, axis=0):
    return tgt.at[idx].add(src)

def _segment_sum(src, seg, n):
    return jax.ops.segment_sum(src, seg, n)
kernel_name = 'mk_cond_seq_d4_seqx_r4_fd4b12'

def setup_inputs(seed: int=0):
    np.random.seed(seed)
    _w = jnp.asarray

    def _rec_inputs():
        import jax
        import jax.numpy as jnp
        _rk = jax.random.key(seed)
        x = 7.22e-05 + 1 * jax.random.normal(jax.random.fold_in(_rk, 1), (8, 512, 256), jnp.float32)
        _lenS = 512 - jax.random.randint(jax.random.fold_in(_rk, 7), (8,), 0, max(1, 512 // 4) + 1, jnp.int32)
        _lenS2 = 512 - jax.random.randint(jax.random.fold_in(_rk, 8), (8,), 0, max(1, 512 // 4) + 1, jnp.int32)
        cond_256 = -0.0209273 + 1.04763 * jax.random.normal(jax.random.fold_in(_rk, 11), (8, 64), jnp.float32)
        return (x, cond_256)
    x, cond_256 = _rec_inputs()

    def _L0_cond_setup():
        import jax, jax.numpy as jnp
        import numpy as np
        from math import sqrt
        D_MODEL = 256
        N_HEADS = 16
        D_T = 64
        D_HID = 4 * D_MODEL
        EPS = 1e-06

        def _rmsnorm(x):
            return x * jax.lax.rsqrt(jnp.mean(x * x, axis=-1, keepdims=True) + EPS)

        def _ada_rmsnorm(x, t, gamma_w, beta_w):
            gamma = (t @ gamma_w.T)[:, None, :]
            beta = (t @ beta_w.T)[:, None, :]
            return gamma * _rmsnorm(x) + beta

        def _attention(x, W_q, W_k, W_v, W_o):
            b, l, dm = x.shape
            d_head = dm // N_HEADS
            scale = sqrt(N_HEADS / dm)

            def split(y):
                return y.reshape(b, l, N_HEADS, d_head).transpose(0, 2, 1, 3)
            q = split(x @ W_q.T)
            k = split(x @ W_k.T)
            v = split(x @ W_v.T)
            attn = jax.nn.softmax(scale * jnp.einsum('bnqd,bnkd->bnqk', q, k), axis=-1)
            o = jnp.einsum('bnqk,bnkd->bnqd', attn, v)
            o = o.transpose(0, 2, 1, 3).reshape(b, l, dm)
            return o @ W_o.T

        def _swiglu(x, gate_w, hidden_w, out_w, out_b):
            return jax.nn.silu(x @ gate_w.T) * (x @ hidden_w.T) @ out_w.T + out_b
        key = jax.random.key(seed)
        ks = jax.random.split(key, 16)
        s = 0.02
        inp = {'x': jax.random.normal(ks[0], (4, 512, D_MODEL), dtype=jnp.float32), 't': jax.random.normal(ks[1], (4, D_T), dtype=jnp.float32), 'attn_gamma_w': jax.random.normal(ks[2], (D_MODEL, D_T), dtype=jnp.float32) * s, 'attn_beta_w': jax.random.normal(ks[3], (D_MODEL, D_T), dtype=jnp.float32) * s, 'W_q': jax.random.normal(ks[4], (D_MODEL, D_MODEL), dtype=jnp.float32) * s, 'W_k': jax.random.normal(ks[5], (D_MODEL, D_MODEL), dtype=jnp.float32) * s, 'W_v': jax.random.normal(ks[6], (D_MODEL, D_MODEL), dtype=jnp.float32) * s, 'W_o': jax.random.normal(ks[7], (D_MODEL, D_MODEL), dtype=jnp.float32) * s, 'attn_alpha_w': jax.random.normal(ks[8], (D_MODEL, D_T), dtype=jnp.float32) * s, 'ffn_gamma_w': jax.random.normal(ks[9], (D_MODEL, D_T), dtype=jnp.float32) * s, 'ffn_beta_w': jax.random.normal(ks[10], (D_MODEL, D_T), dtype=jnp.float32) * s, 'gate_w': jax.random.normal(ks[11], (D_HID, D_MODEL), dtype=jnp.float32) * s, 'hidden_w': jax.random.normal(ks[12], (D_HID, D_MODEL), dtype=jnp.float32) * s, 'out_w': jax.random.normal(ks[13], (D_MODEL, D_HID), dtype=jnp.float32) * s, 'out_b': jnp.zeros((D_MODEL,), dtype=jnp.float32), 'ffn_alpha_w': jax.random.normal(ks[14], (D_MODEL, D_T), dtype=jnp.float32) * s}
        return inp
    _L0_cond_all = _L0_cond_setup()
    _L0_cond_in = {k: v for k, v in _L0_cond_all.items() if k in ('attn_gamma_w', 'attn_beta_w', 'W_q', 'W_k', 'W_v', 'W_o', 'attn_alpha_w', 'ffn_gamma_w', 'ffn_beta_w', 'gate_w', 'hidden_w', 'out_w', 'out_b', 'ffn_alpha_w')}
    del _L0_cond_all

    def _L1_cond_setup():
        import jax, jax.numpy as jnp
        import numpy as np
        EPS = 1e-06

        def act_quant(x):
            scale = 127.0 / jnp.clip(jnp.max(jnp.abs(x), axis=-1, keepdims=True), 1e-05, None)
            return jnp.clip(jnp.round(x * scale), -128.0, 127.0) / scale

        def weight_quant(w):
            scale = 1.0 / jnp.clip(jnp.mean(jnp.abs(w)), 1e-05, None)
            return jnp.clip(jnp.round(w * scale), -1.0, 1.0) / scale
        key = jax.random.key(seed)
        k0, k1, k2, k3, k4 = jax.random.split(key, 5)
        B, S, D, FF, C = (4, 1024, 256, 1024, 64)
        return {'x': jax.random.normal(k0, (B, S, D), jnp.float32), 'cond': jax.random.normal(k1, (B, C), jnp.float32), 'norm_w': jax.random.normal(k2, (D, C), jnp.float32) * 0.02, 'up_w': jax.random.normal(k3, (2 * FF, D), jnp.float32) * 0.02, 'down_w': jax.random.normal(k4, (D, FF), jnp.float32) * 0.02}
    _L1_cond_all = _L1_cond_setup()
    _L1_cond_in = {k: v for k, v in _L1_cond_all.items() if k in ('norm_w', 'up_w', 'down_w')}
    del _L1_cond_all

    def _L2_cond_setup():
        import jax, jax.numpy as jnp
        import numpy as np
        DIM = 256
        BN = 128
        H = 64
        DELTA_SCALE = 0.1
        key = jax.random.key(seed)
        ks = jax.random.split(key, 10)
        B, L = (16, 512)

        def init(k, shape, fan_in):
            bound = 1.0 / np.sqrt(fan_in)
            return jax.random.uniform(k, shape, jnp.float32, -bound, bound)
        return {'x': jax.random.normal(ks[0], (B, L, DIM), jnp.float32), 'h_lang': jax.random.normal(ks[1], (B, H), jnp.float32), 'Wd': init(ks[2], (BN, DIM), DIM), 'bd': init(ks[3], (BN,), DIM), 'Wu': init(ks[4], (DIM, BN), BN), 'bu': init(ks[5], (DIM,), BN), 'Wdd': init(ks[6], (BN * DIM, H), H), 'bdd': init(ks[7], (BN * DIM,), H), 'Wdu': init(ks[8], (DIM * BN, H), H), 'bdu': init(ks[9], (DIM * BN,), H)}
    _L2_cond_all = _L2_cond_setup()
    _L2_cond_in = {k: v for k, v in _L2_cond_all.items() if k in ('Wd', 'bd', 'Wu', 'bu', 'Wdd', 'bdd', 'Wdu', 'bdu')}
    del _L2_cond_all

    def _L3_cond_setup():
        import jax, jax.numpy as jnp
        import numpy as np
        EPS = 1e-05
        key = jax.random.key(seed)
        k1, k2, k3, k4 = jax.random.split(key, 4)
        b, t, d, num_con = (8, 1024, 256, 64)
        return {'input': jax.random.normal(k1, (b, t, d), dtype=jnp.float32), 'convInfo': jax.random.normal(k2, (b, num_con), dtype=jnp.float32), 'weight': jnp.ones((d,), dtype=jnp.float32), 'bias': jnp.zeros((d,), dtype=jnp.float32), 'lin_w': jax.random.normal(k3, (d, num_con), dtype=jnp.float32) * (1.0 / np.sqrt(num_con)), 'lin_b': jax.random.normal(k4, (d,), dtype=jnp.float32) * 0.01}
    _L3_cond_all = _L3_cond_setup()
    _L3_cond_in = {k: v for k, v in _L3_cond_all.items() if k in ('weight', 'bias', 'lin_w', 'lin_b')}
    del _L3_cond_all
    return {'x': x, 'cond_256': cond_256, 'L0_cond_attn_gamma_w': _L0_cond_in['attn_gamma_w'], 'L0_cond_attn_beta_w': _L0_cond_in['attn_beta_w'], 'L0_cond_W_q': _L0_cond_in['W_q'], 'L0_cond_W_k': _L0_cond_in['W_k'], 'L0_cond_W_v': _L0_cond_in['W_v'], 'L0_cond_W_o': _L0_cond_in['W_o'], 'L0_cond_attn_alpha_w': _L0_cond_in['attn_alpha_w'], 'L0_cond_ffn_gamma_w': _L0_cond_in['ffn_gamma_w'], 'L0_cond_ffn_beta_w': _L0_cond_in['ffn_beta_w'], 'L0_cond_gate_w': _L0_cond_in['gate_w'], 'L0_cond_hidden_w': _L0_cond_in['hidden_w'], 'L0_cond_out_w': _L0_cond_in['out_w'], 'L0_cond_out_b': _L0_cond_in['out_b'], 'L0_cond_ffn_alpha_w': _L0_cond_in['ffn_alpha_w'], 'L1_cond_norm_w': _L1_cond_in['norm_w'], 'L1_cond_up_w': _L1_cond_in['up_w'], 'L1_cond_down_w': _L1_cond_in['down_w'], 'L2_cond_Wd': _L2_cond_in['Wd'], 'L2_cond_bd': _L2_cond_in['bd'], 'L2_cond_Wu': _L2_cond_in['Wu'], 'L2_cond_bu': _L2_cond_in['bu'], 'L2_cond_Wdd': _L2_cond_in['Wdd'], 'L2_cond_bdd': _L2_cond_in['bdd'], 'L2_cond_Wdu': _L2_cond_in['Wdu'], 'L2_cond_bdu': _L2_cond_in['bdu'], 'L3_cond_weight': _L3_cond_in['weight'], 'L3_cond_bias': _L3_cond_in['bias'], 'L3_cond_lin_w': _L3_cond_in['lin_w'], 'L3_cond_lin_b': _L3_cond_in['lin_b']}

def reference(x, cond_256, L0_cond_attn_gamma_w, L0_cond_attn_beta_w, L0_cond_W_q, L0_cond_W_k, L0_cond_W_v, L0_cond_W_o, L0_cond_attn_alpha_w, L0_cond_ffn_gamma_w, L0_cond_ffn_beta_w, L0_cond_gate_w, L0_cond_hidden_w, L0_cond_out_w, L0_cond_out_b, L0_cond_ffn_alpha_w, L1_cond_norm_w, L1_cond_up_w, L1_cond_down_w, L2_cond_Wd, L2_cond_bd, L2_cond_Wu, L2_cond_bu, L2_cond_Wdd, L2_cond_bdd, L2_cond_Wdu, L2_cond_bdu, L3_cond_weight, L3_cond_bias, L3_cond_lin_w, L3_cond_lin_b):
    import jax
    import jax.numpy as jnp

    def _L0_cond_ref(x, t, attn_gamma_w, attn_beta_w, W_q, W_k, W_v, W_o, attn_alpha_w, ffn_gamma_w, ffn_beta_w, gate_w, hidden_w, out_w, out_b, ffn_alpha_w):
        import jax, jax.numpy as jnp
        import numpy as np
        from math import sqrt
        D_MODEL = 256
        N_HEADS = 16
        D_T = 64
        D_HID = 4 * D_MODEL
        EPS = 1e-06

        def _rmsnorm(x):
            return x * jax.lax.rsqrt(jnp.mean(x * x, axis=-1, keepdims=True) + EPS)

        def _ada_rmsnorm(x, t, gamma_w, beta_w):
            gamma = (t @ gamma_w.T)[:, None, :]
            beta = (t @ beta_w.T)[:, None, :]
            return gamma * _rmsnorm(x) + beta

        def _attention(x, W_q, W_k, W_v, W_o):
            b, l, dm = x.shape
            d_head = dm // N_HEADS
            scale = sqrt(N_HEADS / dm)

            def split(y):
                return y.reshape(b, l, N_HEADS, d_head).transpose(0, 2, 1, 3)
            q = split(x @ W_q.T)
            k = split(x @ W_k.T)
            v = split(x @ W_v.T)
            attn = jax.nn.softmax(scale * jnp.einsum('bnqd,bnkd->bnqk', q, k), axis=-1)
            o = jnp.einsum('bnqk,bnkd->bnqd', attn, v)
            o = o.transpose(0, 2, 1, 3).reshape(b, l, dm)
            return o @ W_o.T

        def _swiglu(x, gate_w, hidden_w, out_w, out_b):
            return jax.nn.silu(x @ gate_w.T) * (x @ hidden_w.T) @ out_w.T + out_b
        a_alpha = (t @ attn_alpha_w.T)[:, None, :]
        x = x + a_alpha * _attention(_ada_rmsnorm(x, t, attn_gamma_w, attn_beta_w), W_q, W_k, W_v, W_o)
        f_alpha = (t @ ffn_alpha_w.T)[:, None, :]
        return x + f_alpha * _swiglu(_ada_rmsnorm(x, t, ffn_gamma_w, ffn_beta_w), gate_w, hidden_w, out_w, out_b)

    def _L1_cond_ref(x, cond, norm_w, up_w, down_w):
        import jax, jax.numpy as jnp
        import numpy as np
        EPS = 1e-06

        def act_quant(x):
            scale = 127.0 / jnp.clip(jnp.max(jnp.abs(x), axis=-1, keepdims=True), 1e-05, None)
            return jnp.clip(jnp.round(x * scale), -128.0, 127.0) / scale

        def weight_quant(w):
            scale = 1.0 / jnp.clip(jnp.mean(jnp.abs(w)), 1e-05, None)
            return jnp.clip(jnp.round(w * scale), -1.0, 1.0) / scale
        scale = cond @ norm_w.T + 1.0
        ms = jnp.mean(x * x, axis=-1, keepdims=True)
        h = x * (scale[:, None, :] * jax.lax.rsqrt(ms + EPS))
        u = h @ up_w.T
        val, gate = jnp.split(u, 2, axis=-1)
        h = val * jax.nn.gelu(gate, approximate=False)
        hq = h + jax.lax.stop_gradient(act_quant(h) - h)
        wq = down_w + jax.lax.stop_gradient(weight_quant(down_w) - down_w)
        y = hq @ wq.T
        return y + x

    def _L2_cond_ref(x, h_lang, Wd, bd, Wu, bu, Wdd, bdd, Wdu, bdu):
        import jax, jax.numpy as jnp
        import numpy as np
        DIM = 256
        BN = 128
        H = 64
        DELTA_SCALE = 0.1
        B, L, D = x.shape
        dWd = ((h_lang @ Wdd.T + bdd) * DELTA_SCALE).reshape(B, BN, D)
        dWu = ((h_lang @ Wdu.T + bdu) * DELTA_SCALE).reshape(B, D, BN)
        Wd_b = Wd + dWd
        Wu_b = Wu + dWu
        down = jax.nn.relu(jnp.einsum('bld,bnd->bln', x, Wd_b) + bd)
        up = jnp.einsum('bln,bdn->bld', down, Wu_b) + bu
        return x + up

    def _L3_cond_ref(input, convInfo, weight, bias, lin_w, lin_b):
        import jax, jax.numpy as jnp
        import numpy as np
        EPS = 1e-05
        mean = jnp.mean(input, axis=-1, keepdims=True)
        var = jnp.mean(jnp.square(input - mean), axis=-1, keepdims=True)
        out = (input - mean) * jax.lax.rsqrt(var + EPS) * weight + bias
        tar_bias = jnp.tanh(convInfo @ lin_w.T + lin_b)[:, None, :]
        out = out + tar_bias
        return out * weight + bias
    x = _L0_cond_ref(x, cond_256, L0_cond_attn_gamma_w, L0_cond_attn_beta_w, L0_cond_W_q, L0_cond_W_k, L0_cond_W_v, L0_cond_W_o, L0_cond_attn_alpha_w, L0_cond_ffn_gamma_w, L0_cond_ffn_beta_w, L0_cond_gate_w, L0_cond_hidden_w, L0_cond_out_w, L0_cond_out_b, L0_cond_ffn_alpha_w)
    x = _L1_cond_ref(x, cond_256, L1_cond_norm_w, L1_cond_up_w, L1_cond_down_w)
    x = _L2_cond_ref(x, cond_256, L2_cond_Wd, L2_cond_bd, L2_cond_Wu, L2_cond_bu, L2_cond_Wdd, L2_cond_bdd, L2_cond_Wdu, L2_cond_bdu)
    x = _L3_cond_ref(x, cond_256, L3_cond_weight, L3_cond_bias, L3_cond_lin_w, L3_cond_lin_b)
    return x

_drawn_inputs = setup_inputs


def setup_inputs(seed=0):
    import zlib

    import numpy as np

    out = dict(_drawn_inputs(seed))
    spreads = {'L0_cond_out_b': (0.0, 2.0), 'L3_cond_weight': (1.0, 0.2), 'L3_cond_bias': (0.0, 0.1)}
    factors = {'L0_cond_attn_gamma_w': 8.0,
     'L0_cond_attn_beta_w': 8.0,
     'L0_cond_W_q': 8.0,
     'L0_cond_W_k': 8.0,
     'L0_cond_W_v': 8.0,
     'L0_cond_W_o': 8.0,
     'L0_cond_attn_alpha_w': 8.0,
     'L0_cond_ffn_gamma_w': 8.0,
     'L0_cond_ffn_beta_w': 8.0,
     'L0_cond_gate_w': 8.0,
     'L0_cond_hidden_w': 8.0,
     'L0_cond_out_w': 8.0,
     'L0_cond_ffn_alpha_w': 3.696,
     'L1_cond_norm_w': 8.0,
     'L1_cond_up_w': 2.707,
     'L1_cond_down_w': 2.71,
     'L2_cond_bd': 177.519,
     'L3_cond_lin_b': 8.0,
     'L2_cond_bu': 64.0}
    for name, (base, spread) in spreads.items():
        noise = np.random.default_rng([zlib.crc32(name.encode()), seed]).standard_normal(out[name].shape)
        drawn = base * np.exp(spread * noise) if base else spread * noise
        out[name] = jnp.asarray(drawn.astype(out[name].dtype))
    for name, factor in factors.items():
        out[name] = (out[name] * factor).astype(out[name].dtype)
    return out
```

```python
from contextlib import ExitStack

import numpy as np
import concourse.bass as bass
from concourse import mybir

F32 = mybir.dt.float32
F32R = mybir.dt.float32r
BF16 = mybir.dt.bfloat16
ALU = mybir.AluOpType
ACT = mybir.ActivationFunctionType
AX = mybir.AxisListType

P = 128
B, T, D = 8, 512, 256
HEADS, HD = 16, 16
NC = 64
FF = 1024
BN = 128
TT = T // P
KC = D // P
FC = FF // P
G = 4
NG = HEADS // G
SLOTS = HEADS // 2
LEAD = 6
SOFTMAX_SCALE = 0.25
RMS_EPS, LN_EPS = 1e-6, 1e-5
DELTA_SCALE = 0.1
ROUND = 1.5 * 2.0 ** 23
HYPER = 2 * BN * D // 2
SLICE = HYPER // B
HN = 256

AG, AB, FG, FB, L1S = range(5)
NV = 5
R_ALPHA_A, R_ALPHA_F, R_ALPHA_F_B, R_L3 = range(4)
NR = 4


class Mark:

    def __init__(self, counter, section, at):
        self.counter, self.section, self.at = counter, section, at


class Counter:

    def __init__(self, prog, sem, step):
        self.prog, self.sem, self.step, self.n, self.pre = prog, sem, step, 0, 0

    def mark(self):
        self.n += self.step
        return Mark(self, self.prog.section, self.n)


class Slot:

    def __init__(self, prog, name):
        self.name, self.free = name, []
        prog.slots.append(self)


class Section:
    def __init__(self, trips):
        self.trips, self.items, self.start, self.total, self.left = trips, {}, {}, {}, {}


class Engine:
    def __init__(self, prog, name, sem):
        self.prog, self.name = prog, name
        self.counter = Counter(prog, sem, 1)
        self.carrier = prog.carrier if name in ("pool", "sp") else None

    def __call__(self, fn, after=(), mark=None, carried=False):
        item = [fn, list(after), None, carried]
        self.prog.section.items.setdefault(self.name, []).append(item)
        self.last = item
        if mark is not None:
            item[2] = mark
            return mark.mark()
        return None

    def mark(self):
        if self.last[2] is None:
            self.last[2] = self.counter
            return self.counter.mark()
        return Mark(self.last[2], self.prog.section, self.last[2].n)

    def wait(self, *marks):
        self.prog.section.items.setdefault(self.name, []).append([None, list(marks), None, True])

    def play(self, e):
        if self.counter.pre:
            e.sem_inc(self.counter.sem, self.counter.pre)
        for section in self.prog.sections:
            items = section.items.get(self.name, [])
            if section.trips:
                for c, n in section.start.items():
                    if n:
                        e.wait_ge(c.sem, c.pre + n)
                if items:
                    with e.Fori(0, section.trips) as i:
                        self.play_items(e, items, section, i)
            else:
                self.play_items(e, items, section, None)

    def play_items(self, e, items, section, i):
        seen = {}
        for fn, marks, raised, carried in items:
            need = {}
            for m, back in [(m, 0) for m in marks if isinstance(m, Mark)] + [
                (m, 1) for s in marks if isinstance(s, str) for m in section.left.get(s, [])
            ]:
                c = m.counter
                if section.trips and m.section is not section:
                    continue
                at = m.at
                if m.section is not section and m.section.trips:
                    at += (m.section.trips - 1) * m.section.total[c]
                if back:
                    at -= section.total[c]
                need[c] = max(need.get(c, at), at)
            for c, at in need.items():
                if at <= seen.get(c, -(10 ** 9)):
                    continue
                seen[c] = at
                e.wait_ge(c.sem, i * section.total[c] + (c.pre + at) if section.trips else c.pre + at)
                if section.trips and (self.carrier is not None or carried):
                    e.sem_inc(self.prog.carrier, 1)
            if fn is not None:
                ins = fn(e, i)
                if raised is not None:
                    ins.then_inc(raised.sem, raised.step)


class Program:

    def __init__(self, nc, ctx):
        self.nc, self.ctx = nc, ctx
        self.slots, self.counters = [], []
        self.carrier = ctx.enter_context(nc.semaphore("carrier"))
        self.sections = [Section(0)]
        self.section = self.sections[0]

    def sem(self, name):
        return self.ctx.enter_context(self.nc.semaphore(name))

    def engine(self, name):
        e = Engine(self, name, self.sem(f"done_{name}"))
        self.counters.append(e.counter)
        return e

    def dma_counter(self, name):
        c = Counter(self, self.sem(f"dma_{name}"), 16)
        self.counters.append(c)
        return c

    def slot(self, name):
        return Slot(self, name)

    def loop(self, trips):
        s = Section(trips)
        s.start = {c: c.n for c in self.counters}
        self.sections.append(s)
        self.section = s
        for slot in self.slots:
            slot.free = [slot.name]

    def end_loop(self):
        s = self.section
        for c in self.counters:
            s.total[c] = c.n - s.start[c]
            c.n = s.start[c] + s.trips * s.total[c]
            if c.step == 1:
                c.pre = max(c.pre, s.total[c])
        for slot in self.slots:
            s.left[slot.name] = [m for m in slot.free if isinstance(m, Mark)]
        self.sections.append(Section(0))
        self.section = self.sections[-1]
        for slot in self.slots:
            slot.free = s.left[slot.name]


def weave(*flows):
    live = [list(f) for f in flows]
    while live:
        for f in list(live):
            for _ in range(f[1]):
                try:
                    next(f[0])
                except StopIteration:
                    live.remove(f)
                    break


def run(flow):
    for _ in flow:
        pass


def cond_seq(nc, x, cond_t, vec_t, row_t, wqk_t, wv_t, wo_t, wg_t, wh_t, wout_t, out_b, wup_t, wdown_t,
             hyper, wd_t, bdd_t, wu_t, bdu_t, bd, bu, lin_b, ln_w, ln_b, out):
    with ExitStack() as ctx:
        prog = Program(nc, ctx)
        pe, act, dve, pool, sp = (prog.engine(n) for n in ("pe", "act", "dve", "pool", "sp"))

        def dram(name, shape, dt):
            return nc.dram_tensor(name, shape, dt, kind="Internal").ap()

        qk_dram = dram("qk_parts", (2, 2, D, T), F32)
        rows_dram = dram("rows", (B, NR * D), F32)
        hyper_dram = dram("hyper_out", (2 * B, HYPER), F32)
        mid_dram = dram("mid", (B, P, TT, D), F32)

        top = ExitStack()

        def sb(name, shape, dt=F32, on=ctx):
            return on.enter_context(nc.sbuf_tensor(name, shape, dt))

        psum = ctx.enter_context(nc.psum_tensor("psum", [P, 8, 512], F32))
        bank = [prog.slot(f"bank{k}") for k in range(8)]

        def mm(out_, lhs, rhs, start, stop, after=(), **kw):
            pe(lambda e, i: e.matmul(out_, lhs, rhs, start=start, stop=stop, **kw), after)

        def transpose(out_, in_, ident_, after=()):
            pe(lambda e, i: e.transpose(out_, in_, ident_), after)

        def activation(out_, in_, func, after=(), **kw):
            act(lambda e, i: e.activation(out_, in_, func, **kw), after)
            return act.mark()

        def copy(eng, out_, in_, after=()):
            if eng is act:
                return activation(out_, in_, ACT.Copy, after)
            eng(lambda e, i: e.tensor_copy(out_, in_), after)
            return eng.mark()

        def tt(eng, out_, a, b, op, after=()):
            eng(lambda e, i: e.tensor_tensor(out_, a, b, op), after)
            return eng.mark()

        def ts(eng, out_, a, s1, s2, op0, op1, after=()):
            eng(lambda e, i: e.tensor_scalar(out_, a, s1, s2, op0, op1), after)
            return eng.mark()

        def dma(counter, dst, src, after=()):
            def start(e, i):
                return e.dma_start(dst(i) if callable(dst) else dst, src(i) if callable(src) else src)
            return sp(start, after, mark=counter)

        def f32(ap):
            return ap.bitcast(F32)

        def fp32_terms(high, low, w_high, w_low):
            return ((high, w_high), (high, w_low), (low, w_high))

        ident = sb("ident", [P, P])
        ident16 = sb("ident16", [P, P], BF16)
        ones = sb("ones", [P, P])
        mhalf = sb("mhalf", [P, TT])
        zero = sb("zero", [P, 1])
        vecs = sb("vecs", [P, NV * KC, B])
        vec = sb("vec", [P, NV * KC])
        hyper_lhs = sb("hyper_lhs", [P, 32])
        down_mean = sb("down_mean", [P, 1])
        bc = sb("bc", [P, 3, D])

        const = {}
        pool(lambda e, i: e.memset(ident[:, :], 0.0))
        m = pool.mark()
        pool(lambda e, i: e.affine_select(out=ident[:, :], in_=ident[:, :], compare_op=ALU.not_equal, fill=1.0,
                                          base=0, pattern=[[-1, P]], channel_multiplier=1), [m])
        m = pool.mark()
        copy(pool, ident16[:, :], ident[:, :], [m])
        pool(lambda e, i: e.memset(ones[:, :], 1.0))
        pool(lambda e, i: e.memset(mhalf[:, :], -0.5))
        pool(lambda e, i: e.memset(zero[:, :], 0.0))
        pool(lambda e, i: e.memset(hyper_lhs[:, :], 0.0))
        const = pool.mark()

        big = ExitStack()
        with ExitStack() as s:
            stage = [sb(f"stage{k}", [P, SLOTS * T], F32, s) for k in range(2)]
        QS = sb("QS", [P, SLOTS, T], F32R, big)
        KS = sb("KS", [P, SLOTS, T], F32R, big)
        Hh = sb("Hh", [P, KC, T], F32R, big)
        Hl = sb("Hl", [P, KC, T], F32R, big)
        H = sb("H", [P, KC * T], F32, big)
        XN = H[:, :].rearrange("p (t d) -> p t d", t=TT)
        Hf = H[:, :].rearrange("p (c t) -> p c t", c=KC)
        XA = sb("XA", [P, TT, D], F32, big)
        X1 = sb("X1", [P, TT, D], F32, big)
        VA = sb("VA", [P, TT, HEADS, 2 * HD], F32, big)
        MR = sb("MR", [8, T], F32R, big)
        NM = sb("NM", [P, NG, TT, G], F32, big)
        NMs = sb("NMs", [P, TT, 8], F32, big)
        ss = sb("ss", [P, TT], F32, big)
        rms = sb("rms", [P, 2, TT], F32, big)
        rec = sb("rec", [P, TT, G], F32, big)
        quant = sb("quant", [P, 2, 4], F32, big)
        HW = sb("HW", [P, G * HN], F32, big)
        HO = sb("HO", [P, HN], F32, big)
        WQKh, WQKl = (sb(f"WQK{n}", [P, KC, 2 * D], F32R, big) for n in "hl")
        WVh, WVl = (sb(f"WV{n}", [P, KC, D], F32R, big) for n in "hl")
        WOh, WOl = (sb(f"WO{n}", [P, KC, D], F32R, big) for n in "hl")
        WGh, WGl = (sb(f"WG{n}", [P, KC, FF], F32R, big) for n in "hl")
        WHh, WHl = (sb(f"WH{n}", [P, KC, FF], F32R, big) for n in "hl")
        WOUTh, WOUTl = (sb(f"WOUT{n}", [P, FC, D], F32R, big) for n in "hl")
        WUPh, WUPl = (sb(f"WUP{n}", [P, KC, 2 * FF], F32R, big) for n in "hl")
        WDN = sb("WDN", [P, FC, D], BF16, big)

        base = nc.sbuf_base
        with ExitStack() as s:
            PR = sb("PR", [P, 2, G, T], F32, s)
        with ExitStack() as s:
            QT = sb("QT", [P, 2, 2, T], F32R, s)
        with ExitStack() as s:
            HV = sb("HV", [P, 2, FF], F32, s)
            Q16 = sb("Q16", [P, 2, FF], BF16, s)
            QT16 = sb("QT16", [P, 2, FC, P], BF16, s)
        sb("hold_first", [P, 2 * G * T], F32, big)
        with ExitStack() as s:
            OA = sb("OA", [P, 2, T], F32, s)
            ON = sb("ON", [P, TT, D], F32, s)
            OTh = sb("OTh", [P, KC, T], F32R, s)
            OTl = sb("OTl", [P, KC, T], F32R, s)
        with ExitStack() as s:
            sb("hold_small", [P, 2 * T + TT * D], F32, s)
            SMALL = sb("SMALL", [P, NV * D], F32, s)
        with ExitStack() as s:
            SG = sb("SG", [P, 2, T], F32, s)
            PP = sb("PP", [P, 2, T], F32, s)
            PPh = sb("PPh", [P, 2, T], F32R, s)
            PPl = sb("PPl", [P, 2, T], F32R, s)
        sb("hold_second", [P, 8 * T], F32, big)

        slot = {n: prog.slot(n) for n in
                ("QS", "KS", "H", "Hparts", "XA", "X1", "VA", "MR", "NMs", "ss", "rms", "rec", "vec", "bc",
                 "HW", "HO", "QT0", "QT1", "PR0", "PR1", "HV0", "HV1", "Q160", "Q161", "QT160", "QT161",
                 "OA0", "OA1", "ON", "OT", "SG0", "SG1", "PP0", "PP1", "PX0", "PX1", "quant0", "quant1",
                 "qk_dram", "mid_dram")}
        c_in, c_x, c_res, c_bc, c_hw, c_ho, c_m, c_mid, c_out = (
            prog.dma_counter(n) for n in ("in", "x", "residual", "rows", "hyper", "hyper_out", "maxima", "mid", "out"))
        c_w = [prog.dma_counter(f"weights{k}") for k in range(2)]
        c_qk = [prog.dma_counter(f"qk_out{k}") for k in range(2)]
        c_stack = prog.dma_counter("stacks")

        stage_free = [[], []]
        loads = [0]

        def split_weights(src, high, low, chunks, n):
            k = loads[0] % 2
            loads[0] += 1
            st = stage[k][:, 0:chunks * n]
            there = dma(c_w[k], st.rearrange("p (c n) -> p c n", c=chunks),
                        src.rearrange("(c p) n -> p c n", p=P), stage_free[k])
            h2, l2 = (w[:, :, :].rearrange("p c n -> p (c n)") for w in (high, low))
            m_high = copy(act, h2, st, [there])
            m_low = tt(dve, l2, st, f32(h2), ALU.subtract, [m_high])
            stage_free[k] = [m_low]
            return m_low

        cond2 = HO[:, 0:B]
        dma(c_in, cond2[0:NC, :], cond_t)
        dma(c_in, cond2[NC:P, :], cond_t)
        small = SMALL[:, 0:NV * D // 2]
        small2 = SMALL[:, NV * D // 2:]
        onf = ON[:, :, :].rearrange("p t d -> p (t d)")
        dma(c_in, small[0:NC, 0:NV * D // 2], vec_t[:, 0:NV * D // 2])
        dma(c_in, small2[0:NC, 0:NV * D // 2], vec_t[:, NV * D // 2:])
        dma(c_in, onf[0:NC, 0:3 * D], row_t)
        rowv = H[0:B, :]
        dma(c_in, rowv[:, 0:D], lin_b.partition_broadcast(B))
        dma(c_in, rowv[:, D:2 * D], ln_w.partition_broadcast(B))
        dma(c_in, rowv[:, 2 * D:3 * D], ln_b.partition_broadcast(B))
        small_in = dma(c_in, rowv[:, 3 * D:4 * D], out_b.partition_broadcast(B))

        copy(dve, hyper_lhs[0:NC, 0:B], cond2[0:NC, :], [small_in, const])
        hyper_ready = copy(dve, hyper_lhs[NC:P, B:2 * B], cond2[NC:P, :])
        half = NV * KC // 2
        for v in range(NV * KC):
            src = small if v < half else small2
            mm(psum[:, 0, v * B:(v + 1) * B], src[0:NC, (v % half) * P:(v % half + 1) * P], cond2[0:NC, :],
               True, True, [small_in])
        for k in range(2):
            n = min(512, 3 * D - 512 * k)
            mm(psum[0:B, 1 + k, 0:n], cond2[0:NC, :], onf[0:NC, 512 * k:512 * k + n], True, True)
        m_tab = pe.mark()
        copy(dve, vecs[:, :, :].rearrange("p v b -> p (v b)"), psum[:, 0, 0:NV * KC * B], [m_tab])
        m_v = dve.mark()
        m_v = ts(dve, vecs[:, L1S * KC:(L1S + 1) * KC, :], vecs[:, L1S * KC:(L1S + 1) * KC, :], 1.0, None,
                 ALU.add, ALU.bypass, [m_v])
        rows = X1[0:B, :, :].rearrange("p t d -> p (t d)")
        copy(dve, rows[:, 0:2 * D], psum[0:B, 1, 0:2 * D])
        tt(dve, rows[:, 2 * D:3 * D], psum[0:B, 1, D:2 * D], rowv[:, 3 * D:4 * D], ALU.mult)
        m = tt(dve, rows[:, 3 * D:4 * D], psum[0:B, 2, 0:D], rowv[:, 0:D], ALU.add)
        m = activation(rows[:, 3 * D:4 * D], rows[:, 3 * D:4 * D], ACT.Tanh, [m])
        m = tt(dve, rows[:, 3 * D:4 * D], rows[:, 3 * D:4 * D], rowv[:, 2 * D:3 * D], ALU.add, [m])
        m = tt(dve, rows[:, 3 * D:4 * D], rows[:, 3 * D:4 * D], rowv[:, D:2 * D], ALU.mult, [m])
        m = tt(dve, rows[:, 3 * D:4 * D], rows[:, 3 * D:4 * D], rowv[:, 2 * D:3 * D], ALU.add, [m])
        rows_there = dma(c_in, rows_dram, rows, [m])
        sp.wait(rows_there)
        slot["H"].free = [m]
        slot["X1"].free = [rows_there]
        slot["HO"].free = [m_tab, hyper_ready]

        va_ones = VA[:, :, :, HD:2 * HD]
        for t in range(TT):
            pool(lambda e, i, t=t: e.memset(VA[:, t, :, HD:2 * HD], 1.0))
        va_init = pool.mark()

        split_weights(wqk_t, WQKh, WQKl, KC, 2 * D)
        qk_ready = split_weights(wv_t, WVh, WVl, KC, D)
        split_weights(wo_t, WOh, WOl, KC, D)
        split_weights(wg_t, WGh, WGl, KC, FF)
        split_weights(wh_t, WHh, WHl, KC, FF)
        split_weights(wout_t, WOUTh, WOUTl, FC, D)
        for n in range(2):
            cols = slice(n * FF, (n + 1) * FF)
            k = loads[0] % 2
            loads[0] += 1
            st = stage[k][:, 0:KC * FF].rearrange("p (c n) -> p c n", c=KC)
            there = dma(c_w[k], st, wup_t[:, cols].rearrange("(c p) n -> p c n", p=P), stage_free[k])
            mh = copy(act, WUPh[:, :, cols], st, [there])
            stage_free[k] = [tt(dve, WUPl[:, :, cols], st, f32(WUPh[:, :, cols]), ALU.subtract, [mh])]

        k = loads[0] % 2
        dw = stage[k][:, 0:FC * D]
        tmp = stage[k][:, FC * D:2 * FC * D]
        there = dma(c_w[k], dw.rearrange("p (c n) -> p c n", c=FC), wdown_t.rearrange("(c p) n -> p c n", p=P),
                    stage_free[k])
        dve(lambda e, i: e.tensor_reduce(quant[:, 0, 0:1], dw, AX.X, ALU.add, apply_absolute_value=True), [there])
        m = dve.mark()
        mm(psum[:, 3, 0:1], ones[:, :], quant[:, 0, 0:1], True, True, [m, const])
        m = pe.mark()
        m = ts(dve, down_mean[:, :], psum[:, 3, 0:1], 1.0 / (D * FF), 1e-5, ALU.mult, ALU.max, [m])
        dve(lambda e, i: e.reciprocal(quant[:, 0, 1:2], down_mean[:, :]), [m])
        m = dve.mark()
        m = ts(dve, tmp, dw, quant[:, 0, 1:2], ROUND, ALU.mult, ALU.add, [m])
        m = ts(dve, tmp, tmp, ROUND, 1.0, ALU.subtract, ALU.min, [m])
        m = ts(dve, WDN[:, :, :].rearrange("p c n -> p (c n)"), tmp, -1.0, None, ALU.max, ALU.bypass, [m])
        stage_free[k] = [m]

        pool(lambda e, i: e.memset(HW[0:2, :], 1.0))
        m = pool.mark()
        for a in range(2):
            for q in range(4):
                dma(c_in, f32(KS[64 * a + 48:64 * a + 50, 2 * q:2 * q + 2, :]),
                    HW[0:2, :].rearrange("p (s t) -> p s t", s=2), [m] + stage_free[0] + stage_free[1])
        ones_there = sp.mark()
        slot["QS"].free = stage_free[0] + stage_free[1]
        slot["KS"].free = slot["QS"].free + [ones_there]
        slot["HW"].free = [ones_there]
        setup_done = [ones_there, va_init, qk_ready]
        pe.wait(*setup_done)

        def norm(src, src_ready, src_reader, gamma, beta, banks, stat_eps=RMS_EPS):
            free = slot["H"].free + slot["ss"].free
            for t in range(TT):
                dve(lambda e, i, t=t: e.tensor_tensor_reduce(
                    out=XN[:, t, :], in0=src[:, t, :], in1=src[:, t, :], scale=1.0, scalar=0.0,
                    op0=ALU.mult, op1=ALU.add, accum_out=ss[:, t:t + 1]), (free + src_ready) if t == 0 else ())
            m = dve.mark()
            m = ts(pool, rms[:, 0, :], ss[:, :], 1.0 / D, stat_eps, ALU.mult, ALU.add, [m] + slot["rms"].free)
            slot["ss"].free = [m]
            m = tt(pool, rms[:, 1, :], rms[:, 0, :], mhalf[:, :], ALU.pow, [m])
            yield
            for t in range(TT):
                ts(dve, XN[:, t, :], src[:, t, :], rms[:, 1, t:t + 1], None, ALU.mult, ALU.bypass, [m])
            m = dve.mark()
            slot["rms"].free = [m]
            src_reader += [m]
            for c in range(KC):
                for t in range(TT):
                    transpose(psum[:, banks[c], t * P:(t + 1) * P], XN[:, t, c * P:(c + 1) * P], ident[:, :],
                              [m] + bank[banks[c]].free)
                up = pe.mark()
                yield
                g = vec[:, gamma * KC + c:gamma * KC + c + 1]
                b = vec[:, beta * KC + c:beta * KC + c + 1] if beta is not None else zero[:, :]
                activation(Hh[:, c, :], psum[:, banks[c], :], ACT.Identity, [up] + slot["Hparts"].free,
                           scale=g, bias=b)
                if c == 0:
                    last_up = []
                last_up.append(up)
                if c == KC - 1:
                    for c2 in range(KC):
                        b2 = vec[:, beta * KC + c2:beta * KC + c2 + 1] if beta is not None else zero[:, :]
                        g2 = vec[:, gamma * KC + c2:gamma * KC + c2 + 1]
                        md = activation(Hf[:, c2, :], psum[:, banks[c2], :], ACT.Identity, last_up, scale=g2, bias=b2)
                        bank[banks[c2]].free = [md]
                        m = tt(dve, Hl[:, c2, :], Hf[:, c2, :], f32(Hh[:, c2, :]), ALU.subtract,
                               [md] + slot["Hparts"].free)
            slot["vec_read"] = md
            slot["H"].free = [m]
            slot["Hready"] = [m]
            yield

        def load_vec(index, after):
            dve(lambda e, i: e.tensor_copy(vec[:, :], vecs[:, :, bass.ds(index(i), 1)].rearrange("p v o -> p (v o)")),
                after)
            return dve.mark()

        def next_batch(i):
            return 0 if i is None else (i + 1) % B

        def norm_next(banks):
            there = dma(c_x, XA[:, :, :], lambda i: x[bass.ds(next_batch(i), 1)].rearrange("o (t p) d -> p (o t) d", p=P)
                        if i is not None else x[0].rearrange("(t p) d -> p t d", p=P), slot["XA"].free)
            mv = load_vec(next_batch, slot["vec"].free)
            readers = []
            act.wait(mv)
            for _ in norm(XA, [there], readers, AG, AB, banks):
                yield
            slot["XA"].free = readers
            slot["vec"].free = [slot["vec_read"]]

        def qkv_next(banks):
            ready = slot["Hready"]
            wrote = []
            for n, m4 in enumerate((0, 2, 1, 3)):
                bk = banks[n % 2]
                cols = slice(m4 * P, (m4 + 1) * P)
                k = 0
                for kc in range(KC):
                    for w, h in ((WQKh, Hh), (WQKh, Hl), (WQKl, Hh)):
                        mm(psum[:, bk, :], w[:, kc, cols], h[:, kc, :], k == 0, k == 5,
                           ready + bank[bk].free if k == 0 else ())
                        k += 1
                m = pe.mark()
                yield
                b = n % 2
                qt = slot[f"QT{b}"]
                mh = activation(QT[:, b, 0, :], psum[:, bk, :], ACT.Copy, [m] + qt.free)
                ml = tt(dve, QT[:, b, 1, :], psum[:, bk, :], f32(QT[:, b, 0, :]), ALU.subtract, [mh])
                bank[bk].free = [ml]
                wq, c = divmod(m4, KC)
                w = dma(c_qk[b], qk_dram[wq, :, c * P:(c + 1) * P, :].rearrange("h p t -> p h t"), f32(QT[:, b, :, :]),
                        [ml] + slot["qk_dram"].free)
                qt.free = [w]
                wrote.append(w)
                S, name = ((QS, "QS"), (KS, "KS"))[wq]
                parts = ((0, 0), (16, 1), (32, 0)) if wq == 0 else ((0, 0), (16, 0), (32, 1))
                for a in range(2):
                    for row, hl in parts:
                        src = qk_dram[wq, hl, c * P:(c + 1) * P, :].rearrange("(s a r) t -> a r s t", a=2, r=HD)[a]
                        dma(c_stack, f32(S[64 * a + row:64 * a + row + HD, 4 * c:4 * c + 4, :]), src, [w] + slot[name].free)
                loaded = Mark(c_stack, prog.section, c_stack.n)
            slot["qk_dram"].free = [loaded]
            slot["stacks_ready"] = [loaded]
            for th in range(TT // 2):
                bk = banks[th % 2]
                for t2 in range(2):
                    t = 2 * th + t2
                    k = 0
                    for kc in range(KC):
                        for h, w in fp32_terms(Hh, Hl, WVh, WVl):
                            mm(psum[:, bk, t2 * D:(t2 + 1) * D], h[:, kc, t * P:(t + 1) * P], w[:, kc, :], k == 0, k == 5,
                               bank[bk].free if k == 0 and t2 == 0 else ())
                            k += 1
                m = pe.mark()
                yield
                m2 = copy(act, VA[:, 2 * th:2 * th + 2, :, 0:HD],
                          psum[:, bk, :].rearrange("p (t h d) -> p t h d", t=2, h=HEADS), [m] + slot["VA"].free)
                bank[bk].free = [m2]
            slot["Hparts"].free = [m]
            slot["V_ready"] = [m2]

        RING = (4, 5, 6)
        ring_at = [0]

        def ring():
            k = RING[ring_at[0] % len(RING)]
            ring_at[0] += 1
            return k

        def maxima(h, state):
            s, a = divmod(h, 2)
            rows_ = slice(64 * a, 64 * a + 48)
            for th in range(2):
                k = 2 * (state["mx"] % 2)
                state["mx"] += 1
                for t2 in range(2):
                    t = 2 * th + t2
                    mm(psum[:, k + t2, :], QS[rows_, s, t * P:(t + 1) * P], KS[rows_, s, :], True, True,
                       state["stacks"] + bank[k].free + bank[k + 1].free)
                m = pe.mark()
                out_ = NM[:, h // G, 2 * th:2 * th + 2, h % G]
                dve(lambda e, i, k=k, out_=out_: e.tensor_reduce(out_, psum[:, k:k + 2, :], AX.X, ALU.max, negate=True),
                    [m])
                r = dve.mark()
                bank[k].free = bank[k + 1].free = [r]
            state["nm"] = r

        def maxima_rows(g, state):
            nm = NM[:, g, :, :].rearrange("p t (s a) -> p t a s", a=2)
            ns = NMs[:, :, :].rearrange("p t (a h s) -> p t a h s", a=2, h=2)
            hi, lo = ns[:, :, :, 0, :], ns[:, :, :, 1, :]
            hi_r = hi.bitcast(F32R)
            m = copy(dve, hi_r, nm, [state["nm"]] + slot["NMs"].free)
            m = tt(dve, lo.bitcast(F32R), nm, hi, ALU.subtract, [m])
            k = ring()
            for t in range(TT):
                transpose(psum[0:8, k, t * P:(t + 1) * P], NMs[:, t, :], ident[:, :], [m] + bank[k].free)
            m = pe.mark()
            slot["NMs"].free = [m]
            m = activation(MR[:, :], psum[0:8, k, :], ACT.Copy, [m] + slot["MR"].free)
            bank[k].free = [m]
            for a in range(2):
                for hl in range(2):
                    r = 64 * a + 48 + hl
                    src = f32(MR[4 * a + 2 * hl:4 * a + 2 * hl + 2, :])
                    dma(c_m, f32(QS[r:r + 1, 2 * g:2 * g + 2, :]), src, [m])
            state["mrow"][g] = [Mark(c_m, prog.section, c_m.n)]
            slot["MR"].free = state["mrow"][g]

        def attention():
            state = {"mx": 0, "stacks": ["stacks_ready"], "mrow": {}, "nm": None}
            for h in range(LEAD):
                maxima(h, state)
                if h % G == G - 1:
                    maxima_rows(h // G, state)
                yield
            pv = None

            def products(g, kc, pr, ready):
                for j in range(G):
                    mm(psum[32 * j:32 * j + 32, 7, :], VA[:, kc, G * g + j, :], PR[:, pr, j, :], kc == 0, kc == TT - 1,
                       ready + (bank[7].free if kc == 0 else []) + ["V_ready"], tile_position=(0, 32 * j))
                m = pe.mark()
                slot[f"PR{pr}"].free = [m]
                return m

            def group_out(g, m):
                b = g % 2
                m = copy(dve, OA[:, b, :], psum[:, 7, :], [m] + slot[f"OA{b}"].free)
                bank[7].free = [m]
                return m

            def group_norm(g, m):
                b = g % 2
                k = ring()
                for t in range(TT):
                    transpose(psum[:, k, t * P:(t + 1) * P], OA[:, b, t * P:(t + 1) * P], ident[:, :],
                              [m] + bank[k].free)
                m = pe.mark()
                slot[f"OA{b}"].free = [m]
                o = psum[:, k, :].rearrange("p (t j d) -> p t j d", t=TT, j=G)
                dve(lambda e, i: e.reciprocal(rec[:, :, :], o[:, :, :, HD]), [m])
                m = dve.mark()
                dst = ON[:, :, g * G * HD:(g + 1) * G * HD].rearrange("p t (j d) -> p t j d", j=G)
                r4 = rec[:, :, :].unsqueeze(3).broadcast_to([P, TT, G, HD])
                m = tt(dve, dst, o[:, :, :, 0:HD], r4, ALU.mult, [m] + (slot["ON"].free if g == 0 else []))
                bank[k].free = [m]
                return m

            pend, evac = None, None
            for step in range(HEADS):
                g, kc = divmod(step, G)
                pr = kc % 2
                for j in range(G):
                    h = G * g + j
                    s, a = divmod(h, 2)
                    rows_ = slice(64 * a, 64 * a + 50)
                    k = ring()
                    mm(psum[:, k, :], KS[rows_, s, kc * P:(kc + 1) * P], QS[rows_, s, :], True, True,
                       state["stacks"] + state["mrow"][g] + bank[k].free)
                    m = pe.mark()
                    e_ = activation(PR[:, pr, j, :], psum[:, k, :], ACT.Exp, [m] + slot[f"PR{pr}"].free,
                                    scale=SOFTMAX_SCALE)
                    bank[k].free = [e_]
                if step + LEAD < HEADS:
                    h = step + LEAD
                    maxima(h, state)
                    if h % G == G - 1:
                        maxima_rows(h // G, state)
                if evac is not None:
                    normed = group_norm(*evac)
                    evac = None
                if pend is not None:
                    m = products(*pend)
                    if pend[1] == TT - 1:
                        evac = (pend[0], group_out(pend[0], m))
                pend = (g, kc, pr, [e_])
                yield
            m = products(*pend)
            slot["VA"].free = [m]
            slot["KS"].free = [m]
            slot["QS"].free = [m]
            slot["attn_pe_done"] = m
            mo = group_out(pend[0], m)
            yield
            normed = group_norm(pend[0], mo)
            slot["ON_ready"] = [normed]
            yield

        def attn_out(tb, ob):
            for c in range(KC):
                for t in range(TT):
                    transpose(psum[:, tb[c], t * P:(t + 1) * P], ON[:, t, c * P:(c + 1) * P], ident[:, :],
                              slot["ON_ready"] + bank[tb[c]].free)
                m = pe.mark()
                mh = activation(OTh[:, c, :], psum[:, tb[c], :], ACT.Copy, [m] + slot["OT"].free)
                ml = tt(dve, OTl[:, c, :], psum[:, tb[c], :], f32(OTh[:, c, :]), ALU.subtract, [mh])
                bank[tb[c]].free = [ml]
            slot["ON"].free = [m]
            yield
            for th in range(2):
                bk = ob[th]
                for t2 in range(2):
                    t = 2 * th + t2
                    k = 0
                    for kc in range(KC):
                        for h, w in fp32_terms(OTh, OTl, WOh, WOl):
                            mm(psum[:, bk, t2 * D:(t2 + 1) * D], h[:, kc, t * P:(t + 1) * P], w[:, kc, :], k == 0, k == 5,
                               [ml] + (bank[bk].free if t2 == 0 else []) if k == 0 else ())
                            k += 1
                m = pe.mark()
                yield
                al = bc[:, R_ALPHA_A:R_ALPHA_A + 1, :].broadcast_to([P, 2, D])
                dst = ON[:, 2 * th:2 * th + 2, :]
                m2 = tt(dve, dst, psum[:, bk, :].rearrange("p (t d) -> p t d", t=2), al, ALU.mult,
                        [m] + slot["ON"].free + slot["bc_ready"])
                bank[bk].free = [m2]
                x1 = X1[:, 2 * th:2 * th + 2, :]
                m2 = tt(dve, x1, x1, dst, ALU.add, [m2] + slot["X1_ready"])
            slot["OT"].free = [m]
            slot["ON"].free = [m2]
            slot["X1_ready"] = [m2]
            yield

        def swiglu():
            ready = slot["Hready"]
            pend = None

            def out_products(f, b, ready_):
                for t in range(TT):
                    bk = 4 + t // 2
                    k = 0
                    for h, w in fp32_terms(PPh, PPl, WOUTh, WOUTl):
                        mm(psum[:, bk, (t % 2) * D:(t % 2 + 1) * D], h[:, b, t * P:(t + 1) * P], w[:, f, :],
                           f == 0 and k == 0 and t % 2 == 0, f == FC - 1 and k == 2, ready_ + (bank[bk].free if f == 0 else []),
                           skip_group_check=True)
                        k += 1
                m = pe.mark()
                slot[f"PX{b}"].free = [m]
                return m

            for f in range(FC):
                b = f % 2
                gb, hb = 2 * b, 2 * b + 1
                cols = slice(f * P, (f + 1) * P)
                marks = []
                for w2, bk in (((WGh, WGl), gb), ((WHh, WHl), hb)):
                    k = 0
                    for kc in range(KC):
                        for w, h in ((w2[0], Hh), (w2[0], Hl), (w2[1], Hh)):
                            mm(psum[:, bk, :], w[:, kc, cols], h[:, kc, :], k == 0, k == 5,
                               ready + bank[bk].free if k == 0 else ())
                            k += 1
                    marks.append(pe.mark())
                m = activation(SG[:, b, :], psum[:, gb, :], ACT.Silu, [marks[0]] + slot[f"SG{b}"].free)
                bank[gb].free = [m]
                m = tt(dve, PP[:, b, :], SG[:, b, :], psum[:, hb, :], ALU.mult, [m, marks[1]] + slot[f"PP{b}"].free)
                bank[hb].free = [m]
                slot[f"SG{b}"].free = [m]
                mh = activation(PPh[:, b, :], PP[:, b, :], ACT.Copy, [m] + slot[f"PX{b}"].free)
                ml = tt(dve, PPl[:, b, :], PP[:, b, :], f32(PPh[:, b, :]), ALU.subtract, [mh])
                slot[f"PP{b}"].free = [ml]
                if pend is not None:
                    out_products(*pend)
                pend = (f, b, [ml])
                yield
            slot["Hparts"].free = [marks[1]]
            m = out_products(*pend)
            yield
            for th in range(2):
                al = bc[:, R_ALPHA_F:R_ALPHA_F + 1, :].broadcast_to([P, 2, D])
                dst = PP[:, th, :].rearrange("p (t d) -> p t d", t=2)
                m2 = tt(dve, dst, psum[:, 4 + th, :].rearrange("p (t d) -> p t d", t=2), al, ALU.mult,
                        [m] + slot[f"PP{th}"].free)
                bank[4 + th].free = [m2]
                x1 = X1[:, 2 * th:2 * th + 2, :]
                m2 = tt(dve, x1, x1, dst, ALU.add, [m2] + slot["X1_ready"])
                slot[f"PP{th}"].free = [m2]
            slot["X1_ready"] = [m2]
            slot["bc"].free = [m2]
            yield

        def geglu():
            ready = slot["Hready"]
            pend = None

            def down(t, b, ready_):
                tb = psum[:, 4, :].bitcast(BF16)
                for f in range(FC):
                    transpose(tb[:, f * P:(f + 1) * P], Q16[:, b, f * P:(f + 1) * P], ident16[:, :],
                              ready_ + bank[4].free)
                m = pe.mark()
                slot[f"Q16{b}"].free = [m]
                m = copy(act, QT16[:, b, :, :].rearrange("p f t -> p (f t)"), tb, [m] + slot[f"QT16{b}"].free)
                bank[4].free = [m]
                return m

            def finish(t, b, ready_):
                for f in range(FC):
                    mm(psum[:, 5, 0:D], QT16[:, b, f, :], WDN[:, f, :], f == 0, f == FC - 1, ready_ + bank[5].free)
                m = pe.mark()
                slot[f"QT16{b}"].free = [m]
                dve(lambda e, i: e.scalar_tensor_tensor(out=X1[:, t, :], in0=psum[:, 5, 0:D], scalar=quant[:, b, 2:3],
                                                        in1=X1[:, t, :], op0=ALU.mult, op1=ALU.add), [m])
                m = dve.mark()
                bank[5].free = [m]
                slot[f"quant{b}"].free = [m]
                return m

            pair = 0
            last = None
            for t in range(TT):
                b = t % 2
                for hf in range(2):
                    gb, vb = 2 * (pair % 2), 2 * (pair % 2) + 1
                    pair += 1
                    marks = []
                    for bk, off in ((gb, FF), (vb, 0)):
                        cols = slice(off + hf * 512, off + hf * 512 + 512)
                        k = 0
                        for kc in range(KC):
                            for h, w in fp32_terms(Hh, Hl, WUPh, WUPl):
                                mm(psum[:, bk, :], h[:, kc, t * P:(t + 1) * P], w[:, kc, cols], k == 0, k == 5,
                                   ready + bank[bk].free if k == 0 else ())
                                k += 1
                        marks.append(pe.mark())
                    hv = HV[:, b, hf * 512:(hf + 1) * 512]
                    m = activation(hv, psum[:, gb, :], ACT.Gelu, [marks[0]] + slot[f"HV{b}"].free)
                    bank[gb].free = [m]
                    m = tt(dve, hv, hv, psum[:, vb, :], ALU.mult, [m, marks[1]])
                    bank[vb].free = [m]
                    if hf == 0 and last is not None:
                        last = (*last[0:2], down(*last))
                    if hf == 1 and last is not None:
                        finish(last[0], last[1], [last[2]])
                    yield
                hv = HV[:, b, :]
                dve(lambda e, i, b=b, hv=hv: e.tensor_reduce(quant[:, b, 0:1], hv, AX.X, ALU.max,
                                                             apply_absolute_value=True), [m] + slot[f"quant{b}"].free)
                m = dve.mark()
                m = ts(dve, quant[:, b, 1:2], quant[:, b, 0:1], 1e-5, 1.0 / 127.0, ALU.max, ALU.mult, [m])
                ts(dve, quant[:, b, 2:3], quant[:, b, 1:2], down_mean[:, :], None, ALU.mult, ALU.bypass, [m])
                dve(lambda e, i, b=b: e.reciprocal(quant[:, b, 3:4], quant[:, b, 1:2]))
                m = dve.mark()
                m = ts(dve, hv, hv, quant[:, b, 3:4], ROUND, ALU.mult, ALU.add, [m])
                m = ts(pool, Q16[:, b, :], hv, ROUND, None, ALU.subtract, ALU.bypass, [m] + slot[f"Q16{b}"].free)
                slot[f"HV{b}"].free = [m]
                last = (t, b, [m])
            slot["Hparts"].free = [marks[1]]
            m = down(*last)
            yield
            m = finish(last[0], last[1], [m])
            there = dma(c_mid, lambda i: mid_dram[bass.ds(i, 1)].rearrange("o p t d -> (o p) t d"), X1[:, :, :], [m])
            slot["X1"].free = [there]
            yield

        def hyper_slice():
            for q in range(SLICE // (G * HN)):
                there = dma(c_hw, HW[:, :], lambda i, q=q: hyper[:, bass.ds(i * SLICE + q * G * HN, G * HN)],
                            slot["HW"].free)
                yield
                bk = 6
                for j in range(G):
                    mm(psum[32 * j:32 * j + 32, bk, 0:HN], hyper_lhs[:, :], HW[:, j * HN:(j + 1) * HN], True, True,
                       [there] + bank[bk].free, tile_position=(0, 32 * j))
                m = pe.mark()
                slot["HW"].free = [m]
                m = copy(act, HO[:, :], psum[:, bk, 0:HN], [m] + slot["HO"].free)
                bank[bk].free = [m]
                for j in range(G):
                    dma(c_ho, lambda i, q=q, j=j: hyper_dram[:, bass.ds(i * SLICE + (q * G + j) * HN, HN)],
                        HO[32 * j:32 * j + 2 * B, :], [m])
                slot["HO"].free = [Mark(c_ho, prog.section, c_ho.n)]
                yield

        extra = {}

        slot_marks = ("stacks_ready", "V_ready")
        slot["vec"].free = [m_v]
        slot["VA"].free = [va_init]
        run(norm_next((0, 1)))
        run(qkv_next((2, 3)))
        for n in slot_marks:
            extra[n] = slot[n]

        prog.loop(B)
        slot["X1_ready"] = [dma(c_res, X1[:, :, :], lambda i: x[bass.ds(i, 1)].rearrange("o (t p) d -> p (o t) d", p=P),
                                slot["X1"].free)]
        slot["bc_ready"] = [dma(c_bc, bc[:, :, :], lambda i: rows_dram[bass.ds(i, 1), 0:3 * D]
                                .rearrange("o (r d) -> o r d", r=3).broadcast_to([P, 3, D]), slot["bc"].free)]
        run(attention())
        run(attn_out((0, 1), (2, 3)))
        mv = load_vec(lambda i: i, slot["vec"].free)
        act.wait(mv)
        run(norm(X1, slot["X1_ready"], [], FG, FB, (0, 1)))
        m = tt(pool, X1[:, :, :], X1[:, :, :], bc[:, R_ALPHA_F_B:R_ALPHA_F_B + 1, :].broadcast_to([P, TT, D]), ALU.add,
               slot["rms"].free)
        slot["X1_ready"] = [m]
        run(swiglu())
        run(norm(X1, slot["X1_ready"], [], L1S, None, (0, 1)))
        slot["vec"].free = [slot["vec_read"]]
        weave((geglu(), 1), (hyper_slice(), 1))
        run(norm_next((0, 1)))
        run(qkv_next((2, 3)))
        for n in slot_marks:
            prog.section.left[n] = slot[n]
        prog.end_loop()
        big.close()
        print_marks = {c.sem: c.n for c in prog.counters}

        x3 = [sb(f"x3_{k}", [P, TT, D]) for k in range(2)]
        xth = [sb(f"xth{k}", [P, KC, T], F32R) for k in range(2)]
        xtl = [sb(f"xtl{k}", [P, KC, T], F32R) for k in range(2)]
        raw = [sb(f"raw{k}", [P, 2, D]) for k in range(2)]
        wb = [sb(f"wb{k}", [P, 2, D]) for k in range(2)]
        wbh = [sb(f"wbh{k}", [P, 2, D], F32R) for k in range(2)]
        wbl = [sb(f"wbl{k}", [P, 2, D], F32R) for k in range(2)]
        dn = [sb(f"dn{k}", [P, T]) for k in range(2)]
        dnh = [sb(f"dnh{k}", [P, T], F32R) for k in range(2)]
        dnl = [sb(f"dnl{k}", [P, T], F32R) for k in range(2)]
        y = [sb(f"y{k}", [P, TT, D]) for k in range(2)]
        l3row = [sb(f"l3row{k}", [P, D]) for k in range(2)]
        stats = [sb(f"stats{k}", [P, TT, 6]) for k in range(2)]
        mv2 = [sb(f"mv{k}", [P, TT, 2]) for k in range(2)]
        rstd = [sb(f"rstd{k}", [P, 2, TT]) for k in range(2)]
        wbase = sb("wbase", [P, 2, D])
        wbias = sb("wbias", [P, 2, D])
        bd_col = sb("bd_col", [P, 1])
        bu_bc = sb("bu_bc", [P, D])
        w2_bc = sb("w2_bc", [P, D])
        c_in2 = prog.dma_counter("in2")
        c_x3 = [prog.dma_counter(f"x3_{k}") for k in range(2)]
        c_y = [prog.dma_counter(f"y_{k}") for k in range(2)]
        names2 = [f"{n}{k}" for n in ("x3", "xt", "raw", "wb", "wbp", "dn", "dnp", "y", "l3", "st") for k in range(2)]
        s2 = {n: prog.slot("t_" + n) for n in names2}

        everything = [Mark(c, prog.sections[0], c.n) for c in prog.counters if c.n]
        for e in (pe, act, dve, pool, sp):
            e.wait(*everything)
        dma(c_in2, wbase[:, 0, :].rearrange("p (c n) -> p c n", c=KC), wd_t.rearrange("(c p) n -> p c n", p=P))
        dma(c_in2, wbase[:, 1, :], wu_t)
        dma(c_in2, wbias[:, 0, :].rearrange("p (c n) -> p c n", c=KC), bdd_t.rearrange("(c p) n -> p c n", p=P))
        dma(c_in2, wbias[:, 1, :], bdu_t)
        dma(c_in2, bd_col[:, :], bd.rearrange("(p o) -> p o", o=1))
        dma(c_in2, bu_bc[:, :], bu.partition_broadcast(P))
        m = dma(c_in2, w2_bc[:, :], ln_w.partition_broadcast(P))
        dve(lambda e, i: e.scalar_tensor_tensor(out=wbase[:, :, :], in0=wbias[:, :, :], scalar=DELTA_SCALE,
                                                in1=wbase[:, :, :], op0=ALU.mult, op1=ALU.add), [m])
        tt(dve, w2_bc[:, :], w2_bc[:, :], w2_bc[:, :], ALU.mult, [m])
        dve.mark()

        prog.loop(B // 2)

        def l2l3(k):
            def at(i):
                return 2 * i + k
            b0 = 4 * k
            xk = x3[k]
            n = c_x3[k]
            free = s2[f"x3{k}"].free + s2[f"raw{k}"].free + s2[f"l3{k}"].free
            dma(n, xk[:, :, :], lambda i: mid_dram[bass.ds(at(i), 1)].rearrange("o p t d -> (o p) t d"), free)
            for kc in range(KC):
                dma(n, raw[k][:, 0, kc * BN:(kc + 1) * BN],
                    lambda i, kc=kc: hyper_dram[bass.ds(at(i) + kc * B, 1), 0:HYPER // 2]
                    .rearrange("o (p n) -> (o p) n", p=P))
                dma(n, raw[k][64 * kc:64 * kc + 64, 1, :],
                    lambda i, kc=kc: hyper_dram[bass.ds(at(i) + kc * B, 1), HYPER // 2:HYPER]
                    .rearrange("o (p n) -> (o p) n", p=64))
            there = dma(n, l3row[k][:, :], lambda i: rows_dram[bass.ds(at(i), 1), 3 * D:4 * D].broadcast_to([P, D]))
            yield
            dve(lambda e, i: e.scalar_tensor_tensor(out=wb[k][:, :, :], in0=raw[k][:, :, :], scalar=DELTA_SCALE,
                                                    in1=wbase[:, :, :], op0=ALU.mult, op1=ALU.add),
                [there] + s2[f"wb{k}"].free)
            m = dve.mark()
            s2[f"raw{k}"].free = [m]
            mh = activation(wbh[k][:, :, :], wb[k][:, :, :], ACT.Copy, [m] + s2[f"wbp{k}"].free)
            w_ready = tt(dve, wbl[k][:, :, :], wb[k][:, :, :], f32(wbh[k][:, :, :]), ALU.subtract, [mh])
            s2[f"wb{k}"].free = [w_ready]
            for c in range(KC):
                bk = b0 + c
                for t in range(TT):
                    transpose(psum[:, bk, t * P:(t + 1) * P], xk[:, t, c * P:(c + 1) * P], ident[:, :],
                              [there] + bank[bk].free)
                m = pe.mark()
                mh = activation(xth[k][:, c, :], psum[:, bk, :], ACT.Copy, [m] + s2[f"xt{k}"].free)
                x_ready = tt(dve, xtl[k][:, c, :], psum[:, bk, :], f32(xth[k][:, c, :]), ALU.subtract, [mh])
                bank[bk].free = [x_ready]
            mp = tt(pool, xk[:, :, :], xk[:, :, :], bu_bc[:, :].unsqueeze(1).broadcast_to([P, TT, D]), ALU.add,
                    [m, there])
            yield
            bk = b0 + 2
            q = 0
            for kc in range(KC):
                cols = slice(kc * BN, (kc + 1) * BN)
                for w, h in ((wbh, xth), (wbh, xtl), (wbl, xth)):
                    mm(psum[:, bk, :], w[k][:, 0, cols], h[k][:, kc, :], q == 0, q == 5,
                       [w_ready, x_ready] + bank[bk].free)
                    q += 1
            m = pe.mark()
            s2[f"xt{k}"].free = [m]
            yield
            m = activation(dn[k][:, :], psum[:, bk, :], ACT.Relu, [m] + s2[f"dn{k}"].free, bias=bd_col[:, :])
            bank[bk].free = [m]
            mh = activation(dnh[k][:, :], dn[k][:, :], ACT.Copy, [m] + s2[f"dnp{k}"].free)
            ml = tt(dve, dnl[k][:, :], dn[k][:, :], f32(dnh[k][:, :]), ALU.subtract, [mh])
            s2[f"dn{k}"].free = [ml]
            for th in range(2):
                bk = b0 + th
                for t2 in range(2):
                    t = 2 * th + t2
                    q = 0
                    for h, w in ((dnh, wbh), (dnh, wbl), (dnl, wbh)):
                        mm(psum[:, bk, t2 * D:(t2 + 1) * D], h[k][:, t * P:(t + 1) * P], w[k][:, 1, :], q == 0, q == 2,
                           [ml] + bank[bk].free)
                        q += 1
                m = pe.mark()
                xt2 = xk[:, 2 * th:2 * th + 2, :]
                m2 = tt(dve, xt2, psum[:, bk, :].rearrange("p (t d) -> p t d", t=2), xt2, ALU.add, [m, mp])
                bank[bk].free = [m2]
            s2[f"dnp{k}"].free = [m]
            s2[f"wbp{k}"].free = [m]
            yield
            for t in range(TT):
                dve(lambda e, i, t=t: e.bn_stats(stats[k][:, t, :], xk[:, t, :]), [m2])
            m = dve.mark()
            for t in range(TT):
                dve(lambda e, i, t=t: e.bn_aggr(mv2[k][:, t, :], stats[k][:, t, :]), [m] + s2[f"st{k}"].free, carried=True)
            m_s = dve.mark()
            m = ts(pool, rstd[k][:, 0, :], mv2[k][:, :, 1], 1.0, LN_EPS, ALU.mult, ALU.add, [m_s] + s2[f"st{k}"].free)
            m = tt(pool, rstd[k][:, 1, :], rstd[k][:, 0, :], mhalf[:, :], ALU.pow, [m])
            for t in range(TT):
                ts(dve, y[k][:, t, :], xk[:, t, :], mv2[k][:, t, 0:1], rstd[k][:, 1, t:t + 1], ALU.subtract, ALU.mult,
                   [m] + s2[f"y{k}"].free)
            m = dve.mark()
            s2[f"x3{k}"].free = [m]
            s2[f"st{k}"].free = [m]
            yield
            m = tt(dve, y[k][:, :, :], y[k][:, :, :], w2_bc[:, :].unsqueeze(1).broadcast_to([P, TT, D]), ALU.mult, [m])
            m = tt(pool, y[k][:, :, :], y[k][:, :, :], l3row[k][:, :].unsqueeze(1).broadcast_to([P, TT, D]), ALU.add, [m])
            s2[f"l3{k}"].free = [m]
            m = dma(c_y[k], lambda i: out[bass.ds(at(i), 1)].rearrange("o (t p) d -> p (o t) d", p=P), y[k][:, :, :], [m])
            s2[f"y{k}"].free = [m]
            yield

        weave((l2l3(0), 1), (l2l3(1), 1))
        prog.end_loop()
        sp.wait(*[Mark(c, prog.sections[0], c.n) for c in c_y])

        block = ctx.enter_context(nc.Block())
        block.sync(sp.play)
        block.gpsimd(pool.play)
        block.scalar(act.play)
        block.vector(dve.play)
        block.tensor(pe.play)


def kernel(x, cond_256, L0_cond_attn_gamma_w, L0_cond_attn_beta_w, L0_cond_W_q, L0_cond_W_k, L0_cond_W_v, L0_cond_W_o,
           L0_cond_attn_alpha_w, L0_cond_ffn_gamma_w, L0_cond_ffn_beta_w, L0_cond_gate_w, L0_cond_hidden_w, L0_cond_out_w,
           L0_cond_out_b, L0_cond_ffn_alpha_w, L1_cond_norm_w, L1_cond_up_w, L1_cond_down_w, L2_cond_Wd, L2_cond_bd,
           L2_cond_Wu, L2_cond_bu, L2_cond_Wdd, L2_cond_bdd, L2_cond_Wdu, L2_cond_bdu, L3_cond_weight, L3_cond_bias,
           L3_cond_lin_w, L3_cond_lin_b):
    import concourse.bacc as bacc
    from concourse.bass_utils import run_bass_kernel_spmd

    def a(v):
        return np.asarray(v)

    def tr(*ws):
        return np.concatenate([a(w) for w in ws], axis=0).T

    wdd = a(L2_cond_Wdd).reshape(BN, D, NC).transpose(2, 1, 0).reshape(NC, 2, -1)
    wdu = a(L2_cond_Wdu).reshape(D, BN, NC).transpose(2, 1, 0).reshape(NC, 2, -1)
    hyper = np.concatenate([wdd, wdu], axis=2).transpose(1, 0, 2).reshape(2 * NC, -1)
    arrays = {
        "x": a(x),
        "cond_t": a(cond_256).T,
        "vec_t": tr(L0_cond_attn_gamma_w, L0_cond_attn_beta_w, L0_cond_ffn_gamma_w, L0_cond_ffn_beta_w, L1_cond_norm_w),
        "row_t": tr(L0_cond_attn_alpha_w, L0_cond_ffn_alpha_w, L3_cond_lin_w),
        "wqk_t": tr(L0_cond_W_q, L0_cond_W_k),
        "wv_t": tr(L0_cond_W_v),
        "wo_t": tr(L0_cond_W_o),
        "wg_t": tr(L0_cond_gate_w),
        "wh_t": tr(L0_cond_hidden_w),
        "wout_t": tr(L0_cond_out_w),
        "out_b": a(L0_cond_out_b),
        "wup_t": tr(L1_cond_up_w),
        "wdown_t": tr(L1_cond_down_w),
        "hyper": hyper,
        "wd_t": tr(L2_cond_Wd),
        "bdd_t": a(L2_cond_bdd).reshape(BN, D).T,
        "wu_t": tr(L2_cond_Wu),
        "bdu_t": a(L2_cond_bdu).reshape(D, BN).T,
        "bd": a(L2_cond_bd),
        "bu": a(L2_cond_bu),
        "lin_b": a(L3_cond_lin_b),
        "ln_w": a(L3_cond_weight),
        "ln_b": a(L3_cond_bias),
    }
    nc = bacc.Bacc("TRN2", target_bir_lowering=False, num_devices=1)
    ins, args = {}, []
    for name, v in arrays.items():
        v = np.ascontiguousarray(v)
        ins["in_" + name] = v
        args.append(nc.dram_tensor("in_" + name, v.shape, mybir.dt.from_np(v.dtype), kind="ExternalInput").ap())
    out = nc.dram_tensor("out", (B, T, D), F32, kind="ExternalOutput").ap()
    cond_seq(nc, *args, out)
    return run_bass_kernel_spmd(nc, [ins], core_ids=[0]).results[0]["out"]
```

```python
from contextlib import ExitStack

import numpy as np
import concourse.bass as bass
from concourse import mybir

F32 = mybir.dt.float32
F32R = mybir.dt.float32r
BF16 = mybir.dt.bfloat16
ALU = mybir.AluOpType
ACT = mybir.ActivationFunctionType
AX = mybir.AxisListType

P = 128
B, T, D = 8, 512, 256
HEADS, HD = 16, 16
NC = 64
FF = 1024
BN = 128
TT = T // P
KC = D // P
FC = FF // P
G = 4
NG = HEADS // G
STACKED = ((0, 0, 1, 1, 0, 2), (0, 1, 0, 1, 2, 0))
STACK = len(STACKED[0]) * HD
LEAD = 8
SOFTMAX_SCALE = 0.25
RMS_EPS, LN_EPS = 1e-6, 1e-5
DELTA_SCALE = 0.1
ROUND = 1.5 * 2.0 ** 23
HYPER = 2 * BN * D // 2
SLICE = HYPER // B
HN = 256

AG, AB, FG, FB, L1S = range(5)
NV = 5
R_ALPHA_A, R_ALPHA_F, R_ALPHA_F_B, R_L3 = range(4)
NR = 4


END = object()


class Mark:

    def __init__(self, counter, section, at):
        self.counter, self.section, self.at = counter, section, at


class Counter:

    def __init__(self, prog, sem, step):
        self.prog, self.sem, self.step, self.n, self.pre = prog, sem, step, 0, 0

    def mark(self):
        self.n += self.step
        return Mark(self, self.prog.section, self.n)


class Slot:

    def __init__(self, prog, name):
        self.name, self.free = name, []
        prog.slots.append(self)


class Section:
    def __init__(self, trips):
        self.trips, self.items, self.start, self.total, self.left = trips, {}, {}, {}, {}


class Engine:
    def __init__(self, prog, name, sem):
        self.prog, self.name = prog, name
        self.counter = Counter(prog, sem, 1)
        self.carrier = prog.carrier if name in ("pool", "sp") else None

    def __call__(self, fn, after=(), mark=None, carried=False):
        item = [fn, list(after), None, carried]
        self.prog.section.items.setdefault(self.name, []).append(item)
        self.last = item
        if mark is not None:
            item[2] = mark
            return mark.mark()
        return None

    def mark(self):
        if self.last[2] is None:
            self.last[2] = self.counter
            return self.counter.mark()
        return Mark(self.last[2], self.prog.section, self.last[2].n)

    def wait(self, *marks):
        self.prog.section.items.setdefault(self.name, []).append([None, list(marks), None, True])

    def play(self, e):
        for c in [self.counter] + [c for c in self.prog.counters if c.step != 1 and self.name == "sp"]:
            if c.pre:
                e.sem_inc(c.sem, c.pre)
        for section in self.prog.sections:
            items = section.items.get(self.name, [])
            if section.trips:
                for c, n in section.start.items():
                    if n:
                        e.wait_ge(c.sem, c.pre + n)
                if items:
                    with e.Fori(0, section.trips) as i:
                        self.play_items(e, items, section, i)
            else:
                self.play_items(e, items, section, None)

    def play_items(self, e, items, section, i):
        seen = {}
        for fn, marks, raised, carried in items:
            need = {}
            for m, back in [(m, 0) for m in marks if isinstance(m, Mark)] + [
                (m, 1) for s in marks if isinstance(s, str) for m in section.left.get(s, [])
            ]:
                c = m.counter
                if section.trips and m.section is not section:
                    continue
                at = m.at
                if m.section is not section and m.section.trips:
                    at += (m.section.trips - 1) * m.section.total[c]
                if back:
                    at -= section.total[c]
                need[c] = max(need.get(c, at), at)
            for c, at in need.items():
                if at <= seen.get(c, -(10 ** 9)):
                    continue
                seen[c] = at
                e.wait_ge(c.sem, i * section.total[c] + (c.pre + at) if section.trips else c.pre + at)
                if section.trips and (self.carrier is not None or carried):
                    e.sem_inc(self.prog.carrier, 1)
            if fn is not None:
                ins = fn(e, i)
                if raised is not None:
                    ins.then_inc(raised.sem, raised.step)


class Program:

    def __init__(self, nc, ctx):
        self.nc, self.ctx = nc, ctx
        self.slots, self.counters = [], []
        self.carrier = ctx.enter_context(nc.semaphore("carrier"))
        self.sections = [Section(0)]
        self.section = self.sections[0]

    def sem(self, name):
        return self.ctx.enter_context(self.nc.semaphore(name))

    def engine(self, name):
        e = Engine(self, name, self.sem(f"done_{name}"))
        self.counters.append(e.counter)
        return e

    def dma_counter(self, name):
        c = Counter(self, self.sem(f"dma_{name}"), 16)
        self.counters.append(c)
        return c

    def slot(self, name):
        return Slot(self, name)

    def loop(self, trips):
        s = Section(trips)
        s.start = {c: c.n for c in self.counters}
        self.sections.append(s)
        self.section = s
        for slot in self.slots:
            slot.free = [slot.name]

    def end_loop(self):
        s = self.section
        for c in self.counters:
            s.total[c] = c.n - s.start[c]
            c.n = s.start[c] + s.trips * s.total[c]
            c.pre = max(c.pre, s.total[c])
        for slot in self.slots:
            s.left[slot.name] = [m for m in slot.free if isinstance(m, Mark)]
        self.sections.append(Section(0))
        self.section = self.sections[-1]
        for slot in self.slots:
            slot.free = s.left[slot.name]


def weave(*flows):
    live = [[f[0], f[1], f[2] if len(f) > 2 else 10 ** 6] for f in flows]
    while live:
        for f in list(live):
            for _ in range(f[1]):
                if next(f[0], END) is END:
                    f[2] = 0
                    break
            f[2] -= 1
            if f[2] <= 0:
                live.remove(f)


def take(flow, n):
    for _ in range(n):
        next(flow, None)


def run(flow):
    for _ in flow:
        pass


def cond_seq(nc, x, cond_t, vec_t, row_t, wqk_t, wv_t, wo_t, wg_t, wh_t, wout_t, out_b, wup_t, wdown_t,
             hyper, wd_t, bdd_t, wu_t, bdu_t, bd, bu, lin_b, ln_w, ln_b, out):
    with ExitStack() as ctx:
        prog = Program(nc, ctx)
        pe, act, dve, pool, sp = (prog.engine(n) for n in ("pe", "act", "dve", "pool", "sp"))

        def dram(name, shape, dt):
            return nc.dram_tensor(name, shape, dt, kind="Internal").ap()

        qk_dram = dram("qk_parts", (2, 3, D, T), BF16)
        rows_dram = dram("rows", (B, NR * D), F32)
        hyper_dram = dram("hyper_out", (2 * B, HYPER), F32)
        mid_dram = dram("mid", (B, P, TT, D), F32)

        def sb(name, shape, dt=F32, on=ctx):
            return on.enter_context(nc.sbuf_tensor(name, shape, dt))

        psum = ctx.enter_context(nc.psum_tensor("psum", [P, 8, 512], F32))
        bank = [prog.slot(f"bank{k}") for k in range(8)]

        def mm(out_, lhs, rhs, start, stop, after=(), **kw):
            pe(lambda e, i: e.matmul(out_, lhs, rhs, start=start, stop=stop, **kw), after)

        def transpose(out_, in_, ident_, after=()):
            pe(lambda e, i: e.transpose(out_, in_, ident_), after)

        def activation(out_, in_, func, after=(), **kw):
            act(lambda e, i: e.activation(out_, in_, func, **kw), after)
            return act.mark()

        def copy(eng, out_, in_, after=()):
            if eng is act:
                return activation(out_, in_, ACT.Copy, after)
            eng(lambda e, i: e.tensor_copy(out_, in_), after)
            return eng.mark()

        def tt(eng, out_, a, b, op, after=()):
            eng(lambda e, i: e.tensor_tensor(out_, a, b, op), after)
            return eng.mark()

        def ts(eng, out_, a, s1, s2, op0, op1, after=()):
            eng(lambda e, i: e.tensor_scalar(out_, a, s1, s2, op0, op1), after)
            return eng.mark()

        def dma(counter, dst, src, after=()):
            def start(e, i):
                return e.dma_start(dst(i) if callable(dst) else dst, src(i) if callable(src) else src)
            return sp(start, after, mark=counter)

        def f32(ap):
            return ap.bitcast(F32)

        def fp32_terms(high, low, w_high, w_low):
            return ((high, w_high), (high, w_low), (low, w_high))

        ident = sb("ident", [P, P])
        ident16 = sb("ident16", [P, P], BF16)
        ones = sb("ones", [P, P])
        mhalf = sb("mhalf", [P, TT])
        zero = sb("zero", [P, 1])
        rounds = sb("rounds", [P, 2])
        vecs = sb("vecs", [P, NV * KC, B])
        vec = sb("vec", [P, NV * KC])
        hyper_lhs = sb("hyper_lhs", [P, 32])
        down_mean = sb("down_mean", [P, 1])
        bc = sb("bc", [P, 3, D])

        const = {}
        pool(lambda e, i: e.memset(ident[:, :], 0.0))
        m = pool.mark()
        pool(lambda e, i: e.affine_select(out=ident[:, :], in_=ident[:, :], compare_op=ALU.not_equal, fill=1.0,
                                          base=0, pattern=[[-1, P]], channel_multiplier=1), [m])
        m = pool.mark()
        copy(pool, ident16[:, :], ident[:, :], [m])
        pool(lambda e, i: e.memset(ones[:, :], 1.0))
        pool(lambda e, i: e.memset(mhalf[:, :], -0.5))
        pool(lambda e, i: e.memset(zero[:, :], 0.0))
        pool(lambda e, i: e.memset(rounds[:, 0:1], ROUND))
        pool(lambda e, i: e.memset(rounds[:, 1:2], -ROUND))
        pool(lambda e, i: e.memset(hyper_lhs[:, :], 0.0))
        const = pool.mark()

        big = ExitStack()
        QS = sb("QS", [P, HEADS, T], BF16, big)
        KS = sb("KS", [P, HEADS, T], BF16, big)
        Hh = sb("Hh", [P, KC, T], F32R, big)
        Hl = sb("Hl", [P, KC, T], F32R, big)
        H = sb("H", [P, KC * T], F32, big)
        XN = H[:, :].rearrange("p (t d) -> p t d", t=TT)
        XA = sb("XA", [P, TT, D], F32, big)
        X1 = sb("X1", [P, TT, D], F32, big)
        VA = sb("VA", [P, TT, HEADS, 2 * HD], F32, big)
        MR = sb("MR", [3 * G, T], BF16, big)
        NM = sb("NM", [P, NG, TT, G], F32, big)
        NMs = sb("NMs", [P, TT, 3, G], F32, big)
        NMr = sb("NMr", [P, TT, G], F32, big)
        NM16 = sb("NM16", [P, TT, G], BF16, big)
        ss = sb("ss", [P, TT], F32, big)
        rms = sb("rms", [P, 2, TT], F32, big)
        rec = sb("rec", [P, TT, G], F32, big)
        quant = sb("quant", [P, 2, 4], F32, big)
        HW = sb("HW", [P, G * HN], F32, big)
        HO = sb("HO", [P, HN], F32, big)
        def split_pair(name, chunks, n):
            high = sb(name + "_high", [P, chunks, n], F32R, big)
            with ExitStack() as s:
                whole = sb(name + "_whole", [P, chunks, n], F32, s)
            return high, sb(name + "_low", [P, chunks, n], F32R, big), whole

        WQKh, WQKl, WQK = split_pair("WQK", KC, 2 * D)
        WVh, WVl, WV = split_pair("WV", KC, D)
        WOh, WOl, WO = split_pair("WO", KC, D)
        WGh, WGl, WG = split_pair("WG", KC, FF)
        WHh, WHl, WH = split_pair("WH", KC, FF)
        WOUTh, WOUTl, WOUT = split_pair("WOUT", FC, D)
        WUPh, WUPl, WUP = split_pair("WUP", KC, 2 * FF)
        WDN = sb("WDN", [P, FC, D], BF16, big)

        base = nc.sbuf_base
        with ExitStack() as s:
            PR = sb("PR", [P, 2, G, T], F32, s)
        with ExitStack() as s:
            QT = sb("QT", [P, 2, 3, T], BF16, s)
            QR = sb("QR", [P, T], F32, s)
            Gh = sb("Gh", [P, KC, T], F32R, s)
            Gl = sb("Gl", [P, KC, T], F32R, s)
        with ExitStack() as s:
            sb("hold_queries", [P, 4 * T], F32, s)
            ROWV = sb("ROWV", [P, 4 * D], F32, s)
        with ExitStack() as s:
            HV = sb("HV", [P, 2, FF], F32, s)
            Q16 = sb("Q16", [P, 2, FF], BF16, s)
            QT16 = sb("QT16", [P, 2, FC, P], BF16, s)
        sb("hold_first", [P, 2 * G * T], F32, big)
        with ExitStack() as s:
            OA = sb("OA", [P, 2, T], F32, s)
            ON = sb("ON", [P, TT, D], F32, s)
            OTh = sb("OTh", [P, KC, T], F32R, s)
            OTl = sb("OTl", [P, KC, T], F32R, s)
        with ExitStack() as s:
            TAB = sb("TAB", [P, (NV + 3) * D], F32, s)
            DW = sb("DW", [P, FC * D], F32, s)
        with ExitStack() as s:
            SG = sb("SG", [P, 2, T], F32, s)
            PP = sb("PP", [P, 2, T], F32, s)
            PPh = sb("PPh", [P, 2, T], F32R, s)
            PPl = sb("PPl", [P, 2, T], F32R, s)
        sb("hold_second", [P, 8 * T], F32, big)

        slot = {n: prog.slot(n) for n in
                ("QS", "KS", "H", "Hparts", "Gparts", "QR", "XA", "X1", "VA", "MR", "NMs", "ss", "rms", "rec", "vec", "bc",
                 "HW", "HO", "QT0", "QT1", "PR0", "PR1", "HV0", "HV1", "Q160", "Q161", "QT160", "QT161",
                 "OA0", "OA1", "ON", "OT", "SG0", "SG1", "PP0", "PP1", "PX0", "PX1", "quant0", "quant1",
                 "qk_dram0", "qk_dram1")}
        c_in, c_rowv, c_x, c_res, c_bc, c_hw, c_ho, c_m, c_mid, c_out = (
            prog.dma_counter(n) for n in ("in", "row_vectors", "x", "residual", "rows", "hyper", "hyper_out", "maxima", "mid", "out"))
        c_w = {n: prog.dma_counter("w_" + n) for n in ("qk", "v", "o", "gate", "hidden", "out", "up", "down")}
        c_qk = [prog.dma_counter(f"qk_out{k}") for k in range(2)]
        c_stack = [prog.dma_counter(f"stacks{k}") for k in range(2)]

        cond2 = HO[:, 0:B]
        dma(c_in, cond2[0:NC, :], cond_t)
        dma(c_in, cond2[NC:P, :], cond_t)
        dma(c_in, TAB[0:NC, 0:NV * D], vec_t)
        tables_in = dma(c_in, TAB[0:NC, NV * D:(NV + 3) * D], row_t)
        slot["XA_ready"] = dma(c_x, XA[:, :, :], x[0].rearrange("(t p) d -> p t d", p=P))

        def load_weights(name, whole, src, queue=sp):
            src = src.rearrange("(c p) n -> p c n", p=P)
            return queue(lambda e, i: e.dma_start(whole, src), mark=c_w[name])

        arrived = {"qk": load_weights("qk", WQK[:, :, :], wqk_t), "v": load_weights("v", WV[:, :, :], wv_t)}
        for n, v in enumerate((lin_b, ln_w, ln_b, out_b)):
            rowv_in = dma(c_rowv, ROWV[0:B, n * D:(n + 1) * D], v.partition_broadcast(B))

        def split_weights(name, high, low, whole, there, eng=dve):
            h2, l2, w2 = (w[:, :, :].rearrange("p c n -> p (c n)") for w in (high, low, whole))
            m_high = copy(act, h2, w2, [there])
            return tt(eng, l2, w2, f32(h2), ALU.subtract, [m_high])

        for t in range(TT):
            pool(lambda e, i, t=t: e.memset(VA[:, t, :, HD:2 * HD], 1.0))
        va_init = pool.mark()
        dve(lambda e, i: e.memset(KS[STACK:STACK + 3, :, :], 1.0))
        ones_there = dve.mark()

        copy(dve, hyper_lhs[0:NC, 0:B], cond2[0:NC, :], [tables_in, const])
        hyper_ready = copy(dve, hyper_lhs[NC:P, B:2 * B], cond2[NC:P, :])
        for v in range(NV * KC):
            mm(psum[:, 0, v * B:(v + 1) * B], TAB[0:NC, v * P:(v + 1) * P], cond2[0:NC, :], True, True, [tables_in])
        m_vec = pe.mark()
        for k in range(2):
            n = min(512, 3 * D - 512 * k)
            mm(psum[0:B, 6 + k, 0:n], cond2[0:NC, :], TAB[0:NC, NV * D + 512 * k:NV * D + 512 * k + n], True, True)
        m_tab = pe.mark()
        m_v = copy(dve, vecs[:, :, :].rearrange("p v b -> p (v b)"), psum[:, 0, 0:NV * KC * B], [m_vec])
        m_v = ts(dve, vecs[:, L1S * KC:(L1S + 1) * KC, :], vecs[:, L1S * KC:(L1S + 1) * KC, :], 1.0, None,
                 ALU.add, ALU.bypass, [m_v])
        slot["vec"].free = [m_v]
        slot["VA"].free = [va_init]
        bank[0].free = [m_v]
        slot["HO"].free = [m_tab, hyper_ready]

        def norm(src, src_ready, src_reader, gamma, beta, banks, to="H"):
            high, low = {"H": (Hh, Hl), "G": (Gh, Gl)}[to]
            inv = {}
            for th in range(TT // 2):
                for t in (2 * th, 2 * th + 1):
                    free = slot["H"].free if t == 0 else []
                    dve(lambda e, i, t=t: e.tensor_tensor_reduce(
                        out=XN[:, t, :], in0=src[:, t, :], in1=src[:, t, :], scale=1.0, scalar=0.0,
                        op0=ALU.mult, op1=ALU.add, accum_out=ss[:, t:t + 1]), src_ready[t] + free + slot["ss"].free)
                two = slice(2 * th, 2 * th + 2)
                m = ts(pool, rms[:, 0, two], ss[:, two], 1.0 / D, RMS_EPS, ALU.mult, ALU.add,
                       [dve.mark()] + slot["rms"].free)
                inv[th] = tt(pool, rms[:, 1, two], rms[:, 0, two], mhalf[:, two], ALU.pow, [m])
            slot["ss"].free = [m]
            yield
            for th in range(TT // 2):
                for t in (2 * th, 2 * th + 1):
                    m = ts(dve, XN[:, t, :], src[:, t, :], rms[:, 1, t:t + 1], None, ALU.mult, ALU.bypass, [inv[th]])
                for c in range(KC):
                    for t in (2 * th, 2 * th + 1):
                        transpose(psum[:, banks[c], t * P:(t + 1) * P], XN[:, t, c * P:(c + 1) * P], ident[:, :],
                                  [m] + bank[banks[c]].free)
                up = pe.mark()
                yield
            slot["rms"].free = [m]
            src_reader += [m]
            whole = H[:, :].rearrange("p (c t) -> p c t", c=KC)
            mh, mw = {}, {}
            for ca in range(KC):
                for c, eng in ((ca, act), (KC - 1 - ca, dve)):
                    g = vec[:, gamma * KC + c:gamma * KC + c + 1]
                    b = vec[:, beta * KC + c:beta * KC + c + 1] if beta is not None else None
                    seen = psum[:, banks[c], :]
                    if eng is act:
                        mh[c] = activation(high[:, c, :], seen, ACT.Identity, [up] + slot[to + "parts"].free
                                           + ([mw[c]] if ca else []), scale=g, bias=zero[:, :] if b is None else b)
                    else:
                        mw[c] = ts(dve, whole[:, c, :], seen, g, b, ALU.mult, ALU.bypass if b is None else ALU.add,
                                   [up] + ([mh[c]] if ca else []))
            yield
            for c in range(KC):
                bank[banks[c]].free = [mh[c], mw[c]]
                ml = tt(dve, low[:, c, :], whole[:, c, :], f32(high[:, c, :]), ALU.subtract,
                        [mh[c], mw[c]] + slot[to + "parts"].free)
            for t in range(TT):
                slot["H_tile"][t] = [ml]
            yield
            slot["vec_read"] = [mh[KC - 1], mw[0]]
            slot["H"].free = [ml]

        def load_vec(index, after):
            dve(lambda e, i: e.tensor_copy(vec[:, :], vecs[:, :, bass.ds(index(i), 1)].rearrange("p v o -> p (v o)")),
                after)
            return dve.mark()

        def next_batch(i):
            return 0 if i is None else (i + 1) % B

        def load_next():
            slot["XA_ready"] = dma(c_x, XA[:, :, :], lambda i: x[bass.ds(next_batch(i), 1)].rearrange("o (t p) d -> p (o t) d", p=P)
                        if i is not None else x[0].rearrange("(t p) d -> p t d", p=P), slot["XA"].free)

        def norm_next(banks):
            mv = load_vec(next_batch, slot["vec"].free)
            readers = []
            act.wait(mv)
            for _ in norm(XA, [[slot["XA_ready"]]] * TT, readers, AG, AB, banks):
                yield
            slot["XA"].free = readers[-1:]
            slot["H_next"] = slot["H_tile"][TT - 1]
            slot["vec"].free = slot["vec_read"]

        def qk_next(half, banks):
            for n, wq in enumerate((0, 1)):
                m4 = wq * KC + half
                bk = banks[n % 2]
                cols = slice(m4 * P, (m4 + 1) * P)
                k = 0
                for kc in range(KC):
                    for w, h in ((WQKh, Hh), (WQKh, Hl), (WQKl, Hh)):
                        mm(psum[:, bk, :], w[:, kc, cols], h[:, kc, :], k == 0, k == 5,
                           slot["H_next"] + bank[bk].free if k == 0 else ())
                        k += 1
                m = pe.mark()
                slot["Hparts"].free = [m]
                yield
                qt = slot[f"QT{n}"]
                m = activation(QT[:, n, 0, :], psum[:, bk, :], ACT.Copy, [m] + qt.free)
                m = tt(dve, QR[:, :], psum[:, bk, :], QT[:, n, 0, :], ALU.subtract, [m] + slot["QR"].free)
                bank[bk].free = [m]
                m = activation(QT[:, n, 1, :], QR[:, :], ACT.Copy, [m])
                ml = tt(dve, QT[:, n, 2, :], QR[:, :], QT[:, n, 1, :], ALU.subtract, [m])
                slot["QR"].free = [ml]
                w = dma(c_qk[n], qk_dram[wq, :, half * P:(half + 1) * P, :].rearrange("h p t -> p h t"), QT[:, n, :, :],
                        [ml] + slot[f"qk_dram{half}"].free)
                qt.free = [w]
                S, name = ((QS, "QS"), (KS, "KS"))[wq]
                for row, part in enumerate(STACKED[wq]):
                    src = qk_dram[wq, part, half * P:(half + 1) * P, :].rearrange("(h r) t -> r h t", r=HD)
                    loaded = dma(c_stack[half], S[row * HD:(row + 1) * HD, 8 * half:8 * half + 8, :], src,
                                 [w] + slot[name].free)
            slot[f"qk_dram{half}"].free = [loaded]
            slot[f"stacks{half}"] = [loaded]
            yield

        def v_next(banks):
            for th in range(TT // 2):
                bk = banks[th % 2]
                for t2 in range(2):
                    t = 2 * th + t2
                    k = 0
                    for kc in range(KC):
                        for h, w in fp32_terms(Hh, Hl, WVh, WVl):
                            mm(psum[:, bk, t2 * D:(t2 + 1) * D], h[:, kc, t * P:(t + 1) * P], w[:, kc, :], k == 0, k == 5,
                               slot["H_next"] + bank[bk].free if k == 0 and t2 == 0 else ())
                            k += 1
                m = pe.mark()
                slot["Hparts"].free = [m]
                m2 = copy(act, VA[:, 2 * th:2 * th + 2, :, 0:HD],
                          psum[:, bk, :].rearrange("p (t h d) -> p t h d", t=2, h=HEADS), [m] + slot["VA"].free)
                bank[bk].free = [m2]
                yield
            slot["V_ready"] = [m2]

        started = [False]

        RING = (4, 5, 6)
        ring_at = [0]

        def ring():
            k = RING[ring_at[0] % len(RING)]
            ring_at[0] += 1
            return k

        def maxima(h, t, k, tiles=2):
            free = [m for b in range(tiles) for m in bank[k + b].free]
            for b in range(tiles):
                mm(psum[:, k + b, :], QS[0:STACK, h, (t + b) * P:(t + b + 1) * P], KS[0:STACK, h, :], True, True,
                   ([f"stacks{h // 8}"] if started[0] else slot[f"stacks{h // 8}"]) + free)
            m = pe.mark()
            out_ = NM[:, h // G, t:t + tiles, h % G]
            dve(lambda e, i: e.tensor_reduce(out_, psum[:, k:k + tiles, :], AX.X, ALU.max, negate=True), [m])
            r = dve.mark()
            for b in range(tiles):
                bank[k + b].free = [r]
            slot["nm"] = r

        def maxima_parts(g):
            m = slot["nm"]
            left = NM[:, g, :, :]
            for part in range(3):
                m = copy(dve, NM16[:, :, :], left, [m] + slot["NMs"].free)
                m = copy(dve, NMs[:, :, part, :], NM16[:, :, :], [m])
                if part < 2:
                    m = tt(dve, NMr[:, :, :], left, NM16[:, :, :], ALU.subtract, [m])
                    left = NMr[:, :, :]
            return m

        def maxima_rows(g, k, m):
            for t in range(TT):
                transpose(psum[0:3 * G, k, t * P:(t + 1) * P], NMs[:, t, :, :].rearrange("p q j -> p (q j)"), ident[:, :],
                          [m] + bank[k].free)
            m = pe.mark()
            slot["NMs"].free = [m]
            m = activation(MR[:, :], psum[0:3 * G, k, :], ACT.Copy, [m] + slot["MR"].free)
            bank[k].free = [m]
            for part in range(3):
                r = STACK + part
                dma(c_m, QS[r:r + 1, G * g:G * g + G, :], MR[G * part:G * part + G, :], [m])
            slot["mrow"][g] = [Mark(c_m, prog.section, c_m.n)]
            slot["MR"].free = slot["mrow"][g]

        def maxima_lead(banks):
            started[0] = False
            rows = None
            for h in range(LEAD):
                for t in range(TT):
                    maxima(h, t, banks[(h * TT + t) % len(banks)], 1)
                    if t == 1 and rows is not None:
                        maxima_rows(*rows)
                        rows = None
                    yield
                if h % G == G - 1:
                    rows = (h // G, banks[0], maxima_parts(h // G))
            maxima_rows(*rows)
            yield

        def attention():
            started[0] = True
            slot["mrow"] = {g: [f"mrow{g}"] for g in range(LEAD // G)}

            def products(g, kc, pr, ready):
                for j in range(G):
                    mm(psum[32 * j:32 * j + 32, 7, :], VA[:, kc, G * g + j, :], PR[:, pr, j, :], kc == 0, kc == TT - 1,
                       ready + (bank[7].free if kc == 0 else []) + ["V_ready"], tile_position=(0, 32 * j))
                m = pe.mark()
                slot[f"PR{pr}"].free = [m]
                return m

            def group_out(g, m):
                b = g % 2
                m = copy(act, OA[:, b, :], psum[:, 7, :], [m] + slot[f"OA{b}"].free)
                bank[7].free = [m]
                return m

            def group_norm(g, m, k):
                b = g % 2
                for t in range(TT):
                    transpose(psum[:, k, t * P:(t + 1) * P], OA[:, b, t * P:(t + 1) * P], ident[:, :],
                              [m] + bank[k].free)
                m = pe.mark()
                slot[f"OA{b}"].free = [m]
                o = psum[:, k, :].rearrange("p (t j d) -> p t j d", t=TT, j=G)
                dve(lambda e, i: e.reciprocal(rec[:, :, :], o[:, :, :, HD]), [m])
                m = dve.mark()
                dst = ON[:, :, g * G * HD:(g + 1) * G * HD].rearrange("p t (j d) -> p t j d", j=G)
                r4 = rec[:, :, :].unsqueeze(3).broadcast_to([P, TT, G, HD])
                m = tt(dve, dst, o[:, :, :, 0:HD], r4, ALU.mult, [m] + (slot["ON"].free if g == 0 else []))
                bank[k].free = [m]
                return m

            def scores(h, kc, pr, j):
                k = ring()
                mm(psum[:, k, :], KS[0:STACK + 3, h, kc * P:(kc + 1) * P], QS[0:STACK + 3, h, :], True, True,
                   [f"stacks{h // 8}"] + slot["mrow"][h // G] + bank[k].free)
                m = pe.mark()
                m = activation(PR[:, pr, j, :], psum[:, k, :], ACT.Exp, [m] + slot[f"PR{pr}"].free, scale=SOFTMAX_SCALE)
                bank[k].free = [m]
                return m

            pend, evac, parts = None, None, None
            for step in range(HEADS):
                g, kc = divmod(step, G)
                pr = kc % 2
                lead = step + LEAD
                scores(G * g, kc, pr, 0)
                scores(G * g + 1, kc, pr, 1)
                if lead < HEADS:
                    maxima(lead, 0, 0)
                scores(G * g + 2, kc, pr, 2)
                if evac is not None:
                    group_norm(*evac, 2)
                    evac = None
                if pend is not None:
                    m = products(*pend)
                    if pend[1] == TT - 1:
                        evac = (pend[0], group_out(pend[0], m))
                done = scores(G * g + 3, kc, pr, 3)
                if parts is not None:
                    maxima_rows(*parts[0:1], ring(), parts[1])
                    parts = None
                if lead < HEADS:
                    maxima(lead, 2, 2)
                    if lead % G == G - 1:
                        parts = (lead // G, maxima_parts(lead // G))
                pend = (g, kc, pr, [done])
                yield
            m = products(*pend)
            slot["VA"].free = slot["KS"].free = slot["QS"].free = [m]
            mo = group_out(pend[0], m)
            yield
            slot["ON_ready"] = [group_norm(pend[0], mo, 6)]
            yield

        def attn_out(tb, ob):
            for c in range(KC):
                for t in range(TT):
                    transpose(psum[:, tb[c], t * P:(t + 1) * P], ON[:, t, c * P:(c + 1) * P], ident[:, :],
                              slot["ON_ready"] + bank[tb[c]].free)
                m = pe.mark()
                mh = activation(OTh[:, c, :], psum[:, tb[c], :], ACT.Copy, [m] + slot["OT"].free)
                ml = tt(dve, OTl[:, c, :], psum[:, tb[c], :], f32(OTh[:, c, :]), ALU.subtract, [mh])
                bank[tb[c]].free = [ml]
            slot["ON"].free = [m]
            yield
            for th in range(2):
                bk = ob[th]
                for t2 in range(2):
                    t = 2 * th + t2
                    k = 0
                    for kc in range(KC):
                        for h, w in fp32_terms(OTh, OTl, WOh, WOl):
                            mm(psum[:, bk, t2 * D:(t2 + 1) * D], h[:, kc, t * P:(t + 1) * P], w[:, kc, :], k == 0, k == 5,
                               [ml] + (bank[bk].free if t2 == 0 else []) if k == 0 else ())
                            k += 1
                m = pe.mark()
                yield
                al = bc[:, R_ALPHA_A:R_ALPHA_A + 1, :].broadcast_to([P, 2, D])
                dst = ON[:, 2 * th:2 * th + 2, :]
                m2 = tt(dve, dst, psum[:, bk, :].rearrange("p (t d) -> p t d", t=2), al, ALU.mult,
                        [m] + slot["ON"].free + slot["bc_ready"])
                bank[bk].free = [m2]
                x1 = X1[:, 2 * th:2 * th + 2, :]
                m2 = tt(dve, x1, x1, dst, ALU.add, [m2] + slot["X1_ready"])
                slot["X1_tile"][2 * th] = slot["X1_tile"][2 * th + 1] = [m2]
            slot["OT"].free = [m]
            slot["ON"].free = [m2]
            yield

        def swiglu():
            ready = slot["H_tile"][TT - 1]
            pend = None

            def out_products(f, b, ready_):
                for t in range(TT):
                    bk = 4 + t // 2
                    k = 0
                    for h, w in fp32_terms(PPh, PPl, WOUTh, WOUTl):
                        mm(psum[:, bk, (t % 2) * D:(t % 2 + 1) * D], h[:, b, t * P:(t + 1) * P], w[:, f, :],
                           f == 0 and k == 0 and t % 2 == 0, f == FC - 1 and k == 2, ready_ + (bank[bk].free if f == 0 else []),
                           skip_group_check=True)
                        k += 1
                    if t % 2:
                        yield
                m = pe.mark()
                slot[f"PX{b}"].free = [m]

            for f in range(FC):
                b = f % 2
                gb, hb = 2 * b, 2 * b + 1
                cols = slice(f * P, (f + 1) * P)
                marks = []
                for w2, bk in (((WGh, WGl), gb), ((WHh, WHl), hb)):
                    k = 0
                    for kc in range(KC):
                        for w, h in ((w2[0], Gh), (w2[0], Gl), (w2[1], Gh)):
                            mm(psum[:, bk, :], w[:, kc, cols], h[:, kc, :], k == 0, k == 5,
                               ready + bank[bk].free if k == 0 else ())
                            k += 1
                    marks.append(pe.mark())
                    if bk == gb:
                        yield
                m = activation(SG[:, b, :], psum[:, gb, :], ACT.Silu, [marks[0]] + slot[f"SG{b}"].free)
                bank[gb].free = [m]
                m = tt(dve, PP[:, b, :], SG[:, b, :], psum[:, hb, :], ALU.mult, [m, marks[1]] + slot[f"PP{b}"].free)
                bank[hb].free = [m]
                slot[f"SG{b}"].free = [m]
                mh = activation(PPh[:, b, :], PP[:, b, :], ACT.Copy, [m] + slot[f"PX{b}"].free)
                ml = tt(dve, PPl[:, b, :], PP[:, b, :], f32(PPh[:, b, :]), ALU.subtract, [mh])
                slot[f"PP{b}"].free = [ml]
                yield
                if pend is not None:
                    yield from out_products(*pend)
                pend = (f, b, [ml])
            slot["Gparts"].free = [marks[1]]
            run(out_products(*pend))
            m = pe.mark()
            for th in range(2):
                al = bc[:, R_ALPHA_F:R_ALPHA_F + 1, :].broadcast_to([P, 2, D])
                dst = PP[:, th, :].rearrange("p (t d) -> p t d", t=2)
                m2 = tt(dve, dst, psum[:, 4 + th, :].rearrange("p (t d) -> p t d", t=2), al, ALU.mult,
                        [m] + slot[f"PP{th}"].free)
                bank[4 + th].free = [m2]
                x1 = X1[:, 2 * th:2 * th + 2, :]
                m2 = tt(dve, x1, x1, dst, ALU.add, [m2] + slot["X1_ready"])
                slot[f"PP{th}"].free = [m2]
                slot["X1_tile"][2 * th] = slot["X1_tile"][2 * th + 1] = [m2]
                yield
            slot["bc"].free = [m2]
            yield

        def geglu():
            pend = None

            def down(t, b, ready_):
                tb = psum[:, 4, :].bitcast(BF16)
                for f in range(FC):
                    transpose(tb[:, f * P:(f + 1) * P], Q16[:, b, f * P:(f + 1) * P], ident16[:, :],
                              ready_ + bank[4].free)
                m = pe.mark()
                slot[f"Q16{b}"].free = [m]
                m = copy(act, QT16[:, b, :, :].rearrange("p f t -> p (f t)"), tb, [m] + slot[f"QT16{b}"].free)
                bank[4].free = [m]
                return m

            def finish(t, b, ready_):
                for f in range(FC):
                    mm(psum[:, 5, 0:D], QT16[:, b, f, :], WDN[:, f, :], f == 0, f == FC - 1, ready_ + bank[5].free)
                m = pe.mark()
                slot[f"QT16{b}"].free = [m]
                dve(lambda e, i: e.scalar_tensor_tensor(out=X1[:, t, :], in0=psum[:, 5, 0:D], scalar=quant[:, b, 2:3],
                                                        in1=X1[:, t, :], op0=ALU.mult, op1=ALU.add), [m])
                m = dve.mark()
                bank[5].free = [m]
                slot[f"quant{b}"].free = [m]
                return m

            pair = 0
            last = older = None
            act.wait(*[m for k in range(2) for m in slot[f"QT{k}"].free])
            for t in range(TT):
                b = t % 2
                for hf in range(2):
                    gb, vb = 2 * (pair % 2), 2 * (pair % 2) + 1
                    pair += 1
                    marks = []
                    ready = slot["H_tile"][t]
                    for bk, off in ((gb, FF), (vb, 0)):
                        cols = slice(off + hf * 512, off + hf * 512 + 512)
                        k = 0
                        for kc in range(KC):
                            for h, w in fp32_terms(Hh, Hl, WUPh, WUPl):
                                mm(psum[:, bk, :], h[:, kc, t * P:(t + 1) * P], w[:, kc, cols], k == 0, k == 5,
                                   ready + bank[bk].free if k == 0 else ())
                                k += 1
                        marks.append(pe.mark())
                    hv = HV[:, b, hf * 512:(hf + 1) * 512]
                    m = activation(hv, psum[:, gb, :], ACT.Gelu, [marks[0]] + slot[f"HV{b}"].free)
                    bank[gb].free = [m]
                    m = tt(dve, hv, hv, psum[:, vb, :], ALU.mult, [m, marks[1]])
                    bank[vb].free = [m]
                    if hf == 0 and older is not None:
                        finish(*older)
                    if hf == 1 and last is not None:
                        older = (*last[0:2], [down(*last)])
                    yield
                hv = HV[:, b, :]
                dve(lambda e, i, b=b, hv=hv: e.tensor_reduce(quant[:, b, 0:1], hv, AX.X, ALU.max,
                                                             apply_absolute_value=True), [m] + slot[f"quant{b}"].free)
                m = dve.mark()
                m = ts(dve, quant[:, b, 1:2], quant[:, b, 0:1], 1e-5, 1.0 / 127.0, ALU.max, ALU.mult, [m])
                ts(dve, quant[:, b, 2:3], quant[:, b, 1:2], down_mean[:, :], None, ALU.mult, ALU.bypass, [m])
                dve(lambda e, i, b=b: e.reciprocal(quant[:, b, 3:4], quant[:, b, 1:2]))
                m = dve.mark()
                m = activation(hv, hv, ACT.Identity, [m], scale=quant[:, b, 3:4], bias=rounds[:, 0:1])
                m = activation(Q16[:, b, :], hv, ACT.Identity, [m] + slot[f"Q16{b}"].free, scale=1.0, bias=rounds[:, 1:2])
                slot[f"HV{b}"].free = [m]
                last = (t, b, [m])
            slot["Hparts"].free = [marks[1]]
            finish(*older)
            yield
            m = down(*last)
            yield
            m = finish(last[0], last[1], [m])
            there = dma(c_mid, lambda i: mid_dram[bass.ds(i, 1)].rearrange("o p t d -> (o p) t d"), X1[:, :, :], [m])
            slot["X1"].free = [there]
            yield

        def hyper_load(q):
            slot["HW_ready"] = [dma(c_hw, HW[:, :], lambda i: hyper[:, bass.ds(i * SLICE + q * G * HN, G * HN)],
                                    slot["HW"].free)]

        def hyper_slice(bk):
            quarters = SLICE // (G * HN)
            for q in range(quarters):
                for j in range(G):
                    mm(psum[32 * j:32 * j + 32, bk, 0:HN], hyper_lhs[:, :], HW[:, j * HN:(j + 1) * HN], True, True,
                       slot["HW_ready"] + bank[bk].free, tile_position=(0, 32 * j))
                m = pe.mark()
                slot["HW"].free = [m]
                if q + 1 < quarters:
                    hyper_load(q + 1)
                m = copy(act, HO[:, :], psum[:, bk, 0:HN], [m] + slot["HO"].free)
                bank[bk].free = [m]
                for j in range(G):
                    dma(c_ho, lambda i, q=q, j=j: hyper_dram[:, bass.ds(i * SLICE + (q * G + j) * HN, HN)],
                        HO[32 * j:32 * j + 2 * B, :], [m])
                slot["HO"].free = [Mark(c_ho, prog.section, c_ho.n)]
                yield

        slot["H_tile"] = [[] for _ in range(TT)]
        slot["X1_tile"] = [[] for _ in range(TT)]
        slot["mrow"] = {}

        run(norm_next((0, 1)))
        for name, whole, src in (("o", WO[:, :, :], wo_t), ("gate", WG[:, :, :], wg_t), ("hidden", WH[:, :, :], wh_t),
                                 ("out", WOUT[:, :, :], wout_t), ("up", WUP[:, :, :], wup_t),
                                 ("down", DW[:, :].rearrange("p (c n) -> p c n", c=FC), wdown_t)):
            arrived[name] = load_weights(name, whole, src, pool)
        pe.wait(split_weights("qk", WQKh, WQKl, WQK, arrived["qk"]))
        pe.wait(split_weights("v", WVh, WVl, WV, arrived["v"]))
        run(qk_next(0, (2, 3)))
        run(qk_next(1, (2, 3)))
        run(v_next((4, 5)))

        rowv = ROWV[0:B, :]
        rows = X1[0:B, :, :].rearrange("p t d -> p (t d)")
        copy(dve, rows[:, 0:2 * D], psum[0:B, 6, 0:2 * D], [m_tab, rowv_in])
        tt(dve, rows[:, 2 * D:3 * D], psum[0:B, 6, D:2 * D], rowv[:, 3 * D:4 * D], ALU.mult)
        m_rows = tt(dve, rows[:, 3 * D:4 * D], psum[0:B, 7, 0:D], rowv[:, 0:D], ALU.add)
        bank[6].free = bank[7].free = [m_rows]
        m = activation(rows[:, 3 * D:4 * D], rows[:, 3 * D:4 * D], ACT.Tanh, [m_rows])
        m = tt(dve, rows[:, 3 * D:4 * D], rows[:, 3 * D:4 * D], rowv[:, 2 * D:3 * D], ALU.add, [m])
        m = tt(dve, rows[:, 3 * D:4 * D], rows[:, 3 * D:4 * D], rowv[:, D:2 * D], ALU.mult, [m])
        m = tt(dve, rows[:, 3 * D:4 * D], rows[:, 3 * D:4 * D], rowv[:, 2 * D:3 * D], ALU.add, [m])
        rows_there = dma(c_in, rows_dram, rows, [m])
        slot["X1"].free = [rows_there]
        sp.wait(rows_there)

        lead = maxima_lead(tuple(range(8)))
        pe.wait(ones_there, va_init)
        act.wait(m_rows)
        for name, high, low, whole in (("o", WOh, WOl, WO), ("gate", WGh, WGl, WG), ("hidden", WHh, WHl, WH),
                                       ("out", WOUTh, WOUTl, WOUT), ("up", WUPh, WUPl, WUP)):
            pe.wait(split_weights(name, high, low, whole, arrived[name], dve if name == "o" else pool))
            take(lead, 4)

        dve(lambda e, i: e.tensor_reduce(quant[:, 0, 0:1], DW[:, :], AX.X, ALU.add, apply_absolute_value=True),
            [arrived["down"]])
        m = dve.mark()
        mm(psum[:, 3, 0:1], ones[:, :], quant[:, 0, 0:1], True, True, [m, const] + bank[3].free)
        m = pe.mark()
        m = ts(dve, down_mean[:, :], psum[:, 3, 0:1], 1.0 / (D * FF), 1e-5, ALU.mult, ALU.max, [m])
        bank[3].free = [m]
        dve(lambda e, i: e.reciprocal(quant[:, 0, 1:2], down_mean[:, :]), [m])
        m = dve.mark()
        m = ts(dve, DW[:, :], DW[:, :], quant[:, 0, 1:2], ROUND, ALU.mult, ALU.add, [m])
        m = ts(dve, DW[:, :], DW[:, :], ROUND, 1.0, ALU.subtract, ALU.min, [m])
        signs_ready = ts(dve, WDN[:, :, :].rearrange("p c n -> p (c n)"), DW[:, :], -1.0, None, ALU.max, ALU.bypass, [m])
        pe.wait(signs_ready)
        run(lead)

        prog.loop(B)
        slot["X1_ready"] = [dma(c_res, X1[:, :, :], lambda i: x[bass.ds(i, 1)].rearrange("o (t p) d -> p (o t) d", p=P),
                                slot["X1"].free)]
        load_next()
        slot["bc_ready"] = [dma(c_bc, bc[:, :, :], lambda i: rows_dram[bass.ds(i, 1), 0:3 * D]
                                .rearrange("o (r d) -> o r d", r=3).broadcast_to([P, 3, D]), slot["bc"].free)]
        hyper_load(0)
        attn = attention()
        take(attn, 10)
        weave((attn, 1, 6), (norm_next((0, 1)), 1))
        qk0, qk1, nv, fin, hyp = qk_next(0, (2, 3)), qk_next(1, (2, 3)), v_next((2, 3)), attn_out((0, 1), (4, 5)), hyper_slice(6)
        take(attn, 1)
        take(qk0, 1)
        take(attn, 1)
        take(qk0, 1)
        take(fin, 1)
        take(qk0, 1)
        take(nv, 1)
        take(fin, 2)
        take(nv, 1)
        take(fin, 1)
        mv = load_vec(lambda i: i, slot["vec"].free)
        act.wait(mv)
        norm2 = norm(X1, slot["X1_tile"], [], FG, FB, (0, 1), "G")
        take(norm2, 1)
        take(qk1, 1)
        take(hyp, 1)
        take(norm2, 2)
        take(qk1, 1)
        take(norm2, 1)
        take(hyp, 1)
        take(norm2, 1)
        take(qk1, 1)
        m = tt(pool, X1[:, :, :], X1[:, :, :], bc[:, R_ALPHA_F_B:R_ALPHA_F_B + 1, :].broadcast_to([P, TT, D]), ALU.add,
               slot["rms"].free)
        slot["X1_ready"] = [m]
        ffn, lead = swiglu(), maxima_lead((6, 7))
        take(ffn, 4)
        weave((ffn, 1, 4 * FC - 6), (lead, 1))
        run(lead)
        run(ffn)
        l1 = geglu()
        norm3 = norm(X1, slot["X1_tile"], [], L1S, None, (0, 1))
        take(norm3, 1)
        take(hyp, 1)
        take(norm3, 4)
        take(l1, 2)
        run(hyp)
        run(l1)
        slot["vec"].free = slot["vec_read"]
        for name in ("stacks0", "stacks1", "V_ready"):
            prog.section.left[name] = slot[name]
        for g in range(LEAD // G):
            prog.section.left[f"mrow{g}"] = slot["mrow"][g]
        prog.end_loop()
        big.close()

        x3 = [sb(f"x3_{k}", [P, TT, D]) for k in range(2)]
        xth = [sb(f"xth{k}", [P, KC, T], F32R) for k in range(2)]
        xtl = [sb(f"xtl{k}", [P, KC, T], F32R) for k in range(2)]
        raw = [sb(f"raw{k}", [P, 2, D]) for k in range(2)]
        wb = [sb(f"wb{k}", [P, 2, D]) for k in range(2)]
        wbh = [sb(f"wbh{k}", [P, 2, D], F32R) for k in range(2)]
        wbl = [sb(f"wbl{k}", [P, 2, D], F32R) for k in range(2)]
        dn = [sb(f"dn{k}", [P, T]) for k in range(2)]
        dnh = [sb(f"dnh{k}", [P, T], F32R) for k in range(2)]
        dnl = [sb(f"dnl{k}", [P, T], F32R) for k in range(2)]
        y = [sb(f"y{k}", [P, TT, D]) for k in range(2)]
        l3row = [sb(f"l3row{k}", [P, D]) for k in range(2)]
        stats = [sb(f"stats{k}", [P, TT, 6]) for k in range(2)]
        mv2 = [sb(f"mv{k}", [P, TT, 2]) for k in range(2)]
        rstd = [sb(f"rstd{k}", [P, 2, TT]) for k in range(2)]
        wbase = sb("wbase", [P, 2, D])
        wbias = sb("wbias", [P, 2, D])
        bd_col = sb("bd_col", [P, 1])
        bu_bc = sb("bu_bc", [P, D])
        w2_bc = sb("w2_bc", [P, D])
        c_in2 = prog.dma_counter("in2")
        c_x3 = [prog.dma_counter(f"x3_{k}") for k in range(2)]
        c_y = [prog.dma_counter(f"y_{k}") for k in range(2)]
        names2 = [f"{n}{k}" for n in ("x3", "xt", "raw", "wb", "wbp", "dn", "dnp", "y", "l3", "st") for k in range(2)]
        s2 = {n: prog.slot("t_" + n) for n in names2}

        everything = [Mark(c, prog.sections[0], c.n) for c in prog.counters if c.n]
        for e in (pe, act, dve, pool, sp):
            e.wait(*everything)
        dma(c_in2, wbase[:, 0, :].rearrange("p (c n) -> p c n", c=KC), wd_t.rearrange("(c p) n -> p c n", p=P))
        dma(c_in2, wbase[:, 1, :], wu_t)
        dma(c_in2, wbias[:, 0, :].rearrange("p (c n) -> p c n", c=KC), bdd_t.rearrange("(c p) n -> p c n", p=P))
        dma(c_in2, wbias[:, 1, :], bdu_t)
        dma(c_in2, bd_col[:, :], bd.rearrange("(p o) -> p o", o=1))
        dma(c_in2, bu_bc[:, :], bu.partition_broadcast(P))
        m = dma(c_in2, w2_bc[:, :], ln_w.partition_broadcast(P))
        dve(lambda e, i: e.scalar_tensor_tensor(out=wbase[:, :, :], in0=wbias[:, :, :], scalar=DELTA_SCALE,
                                                in1=wbase[:, :, :], op0=ALU.mult, op1=ALU.add), [m])
        tt(dve, w2_bc[:, :], w2_bc[:, :], w2_bc[:, :], ALU.mult, [m])
        dve.mark()

        prog.loop(B // 2)

        def l2l3(k):
            def at(i):
                return 2 * i + k
            b0 = 4 * k
            xk = x3[k]
            n = c_x3[k]
            free = s2[f"x3{k}"].free + s2[f"raw{k}"].free + s2[f"l3{k}"].free
            dma(n, xk[:, :, :], lambda i: mid_dram[bass.ds(at(i), 1)].rearrange("o p t d -> (o p) t d"), free)
            for kc in range(KC):
                dma(n, raw[k][:, 0, kc * BN:(kc + 1) * BN],
                    lambda i, kc=kc: hyper_dram[bass.ds(at(i) + kc * B, 1), 0:HYPER // 2]
                    .rearrange("o (p n) -> (o p) n", p=P))
                dma(n, raw[k][64 * kc:64 * kc + 64, 1, :],
                    lambda i, kc=kc: hyper_dram[bass.ds(at(i) + kc * B, 1), HYPER // 2:HYPER]
                    .rearrange("o (p n) -> (o p) n", p=64))
            there = dma(n, l3row[k][:, :], lambda i: rows_dram[bass.ds(at(i), 1), 3 * D:4 * D].broadcast_to([P, D]))
            yield
            dve(lambda e, i: e.scalar_tensor_tensor(out=wb[k][:, :, :], in0=raw[k][:, :, :], scalar=DELTA_SCALE,
                                                    in1=wbase[:, :, :], op0=ALU.mult, op1=ALU.add),
                [there] + s2[f"wb{k}"].free)
            m = dve.mark()
            s2[f"raw{k}"].free = [m]
            mh = activation(wbh[k][:, :, :], wb[k][:, :, :], ACT.Copy, [m] + s2[f"wbp{k}"].free)
            w_ready = tt(dve, wbl[k][:, :, :], wb[k][:, :, :], f32(wbh[k][:, :, :]), ALU.subtract, [mh])
            s2[f"wb{k}"].free = [w_ready]
            for c in range(KC):
                bk = b0 + c
                for t in range(TT):
                    transpose(psum[:, bk, t * P:(t + 1) * P], xk[:, t, c * P:(c + 1) * P], ident[:, :],
                              [there] + bank[bk].free)
                m = pe.mark()
                mh = activation(xth[k][:, c, :], psum[:, bk, :], ACT.Copy, [m] + s2[f"xt{k}"].free)
                x_ready = tt(dve, xtl[k][:, c, :], psum[:, bk, :], f32(xth[k][:, c, :]), ALU.subtract, [mh])
                bank[bk].free = [x_ready]
            mp = tt(pool, xk[:, :, :], xk[:, :, :], bu_bc[:, :].unsqueeze(1).broadcast_to([P, TT, D]), ALU.add,
                    [m, there])
            yield
            bk = b0 + 2
            q = 0
            for kc in range(KC):
                cols = slice(kc * BN, (kc + 1) * BN)
                for w, h in ((wbh, xth), (wbh, xtl), (wbl, xth)):
                    mm(psum[:, bk, :], w[k][:, 0, cols], h[k][:, kc, :], q == 0, q == 5,
                       [w_ready, x_ready] + bank[bk].free)
                    q += 1
            m = pe.mark()
            s2[f"xt{k}"].free = [m]
            yield
            m = activation(dn[k][:, :], psum[:, bk, :], ACT.Relu, [m] + s2[f"dn{k}"].free, bias=bd_col[:, :])
            bank[bk].free = [m]
            mh = activation(dnh[k][:, :], dn[k][:, :], ACT.Copy, [m] + s2[f"dnp{k}"].free)
            ml = tt(dve, dnl[k][:, :], dn[k][:, :], f32(dnh[k][:, :]), ALU.subtract, [mh])
            s2[f"dn{k}"].free = [ml]
            for th in range(2):
                bk = b0 + th
                for t2 in range(2):
                    t = 2 * th + t2
                    q = 0
                    for h, w in ((dnh, wbh), (dnh, wbl), (dnl, wbh)):
                        mm(psum[:, bk, t2 * D:(t2 + 1) * D], h[k][:, t * P:(t + 1) * P], w[k][:, 1, :], q == 0, q == 2,
                           [ml] + bank[bk].free)
                        q += 1
                m = pe.mark()
                xt2 = xk[:, 2 * th:2 * th + 2, :]
                m2 = tt(dve, xt2, psum[:, bk, :].rearrange("p (t d) -> p t d", t=2), xt2, ALU.add, [m, mp])
                bank[bk].free = [m2]
            s2[f"dnp{k}"].free = [m]
            s2[f"wbp{k}"].free = [m]
            yield
            for t in range(TT):
                dve(lambda e, i, t=t: e.bn_stats(stats[k][:, t, :], xk[:, t, :]), [m2])
            m = dve.mark()
            for t in range(TT):
                dve(lambda e, i, t=t: e.bn_aggr(mv2[k][:, t, :], stats[k][:, t, :]), [m] + s2[f"st{k}"].free, carried=True)
            m_s = dve.mark()
            m = ts(pool, rstd[k][:, 0, :], mv2[k][:, :, 1], 1.0, LN_EPS, ALU.mult, ALU.add, [m_s] + s2[f"st{k}"].free)
            m = tt(pool, rstd[k][:, 1, :], rstd[k][:, 0, :], mhalf[:, :], ALU.pow, [m])
            for t in range(TT):
                ts(dve, y[k][:, t, :], xk[:, t, :], mv2[k][:, t, 0:1], rstd[k][:, 1, t:t + 1], ALU.subtract, ALU.mult,
                   [m] + s2[f"y{k}"].free)
            m = dve.mark()
            s2[f"x3{k}"].free = [m]
            s2[f"st{k}"].free = [m]
            yield
            m = tt(dve, y[k][:, :, :], y[k][:, :, :], w2_bc[:, :].unsqueeze(1).broadcast_to([P, TT, D]), ALU.mult, [m])
            m = tt(pool, y[k][:, :, :], y[k][:, :, :], l3row[k][:, :].unsqueeze(1).broadcast_to([P, TT, D]), ALU.add, [m])
            s2[f"l3{k}"].free = [m]
            m = dma(c_y[k], lambda i: out[bass.ds(at(i), 1)].rearrange("o (t p) d -> p (o t) d", p=P), y[k][:, :, :], [m])
            s2[f"y{k}"].free = [m]
            yield

        weave((l2l3(0), 1), (l2l3(1), 1))
        prog.end_loop()
        sp.wait(*[Mark(c, prog.sections[0], c.n) for c in c_y])

        block = ctx.enter_context(nc.Block())
        block.sync(sp.play)
        block.gpsimd(pool.play)
        block.scalar(act.play)
        block.vector(dve.play)
        block.tensor(pe.play)


def kernel(x, cond_256, L0_cond_attn_gamma_w, L0_cond_attn_beta_w, L0_cond_W_q, L0_cond_W_k, L0_cond_W_v, L0_cond_W_o,
           L0_cond_attn_alpha_w, L0_cond_ffn_gamma_w, L0_cond_ffn_beta_w, L0_cond_gate_w, L0_cond_hidden_w, L0_cond_out_w,
           L0_cond_out_b, L0_cond_ffn_alpha_w, L1_cond_norm_w, L1_cond_up_w, L1_cond_down_w, L2_cond_Wd, L2_cond_bd,
           L2_cond_Wu, L2_cond_bu, L2_cond_Wdd, L2_cond_bdd, L2_cond_Wdu, L2_cond_bdu, L3_cond_weight, L3_cond_bias,
           L3_cond_lin_w, L3_cond_lin_b):
    import concourse.bacc as bacc
    from concourse.bass_utils import run_bass_kernel_spmd

    def a(v):
        return np.asarray(v)

    def tr(*ws):
        return np.concatenate([a(w) for w in ws], axis=0).T

    wdd = a(L2_cond_Wdd).reshape(BN, D, NC).transpose(2, 1, 0).reshape(NC, 2, -1)
    wdu = a(L2_cond_Wdu).reshape(D, BN, NC).transpose(2, 1, 0).reshape(NC, 2, -1)
    hyper = np.concatenate([wdd, wdu], axis=2).transpose(1, 0, 2).reshape(2 * NC, -1)
    arrays = {
        "x": a(x),
        "cond_t": a(cond_256).T,
        "vec_t": tr(L0_cond_attn_gamma_w, L0_cond_attn_beta_w, L0_cond_ffn_gamma_w, L0_cond_ffn_beta_w, L1_cond_norm_w),
        "row_t": tr(L0_cond_attn_alpha_w, L0_cond_ffn_alpha_w, L3_cond_lin_w),
        "wqk_t": tr(L0_cond_W_q, L0_cond_W_k),
        "wv_t": tr(L0_cond_W_v),
        "wo_t": tr(L0_cond_W_o),
        "wg_t": tr(L0_cond_gate_w),
        "wh_t": tr(L0_cond_hidden_w),
        "wout_t": tr(L0_cond_out_w),
        "out_b": a(L0_cond_out_b),
        "wup_t": tr(L1_cond_up_w),
        "wdown_t": tr(L1_cond_down_w),
        "hyper": hyper,
        "wd_t": tr(L2_cond_Wd),
        "bdd_t": a(L2_cond_bdd).reshape(BN, D).T,
        "wu_t": tr(L2_cond_Wu),
        "bdu_t": a(L2_cond_bdu).reshape(D, BN).T,
        "bd": a(L2_cond_bd),
        "bu": a(L2_cond_bu),
        "lin_b": a(L3_cond_lin_b),
        "ln_w": a(L3_cond_weight),
        "ln_b": a(L3_cond_bias),
    }
    nc = bacc.Bacc("TRN2", target_bir_lowering=False, num_devices=1)
    ins, args = {}, []
    for name, v in arrays.items():
        v = np.ascontiguousarray(v)
        ins["in_" + name] = v
        args.append(nc.dram_tensor("in_" + name, v.shape, mybir.dt.from_np(v.dtype), kind="ExternalInput").ap())
    out = nc.dram_tensor("out", (B, T, D), F32, kind="ExternalOutput").ap()
    cond_seq(nc, *args, out)
    return run_bass_kernel_spmd(nc, [ins], core_ids=[0]).results[0]["out"]
```

```python
from contextlib import ExitStack

import numpy as np
import concourse.bass as bass
from concourse import mybir

F32 = mybir.dt.float32
F32R = mybir.dt.float32r
BF16 = mybir.dt.bfloat16
ALU = mybir.AluOpType
ACT = mybir.ActivationFunctionType
AX = mybir.AxisListType

P = 128
B, T, D = 8, 512, 256
HEADS, HD = 16, 16
NC = 64
FF = 1024
BN = 128
TT = T // P
KC = D // P
FC = FF // P
G = 4
NG = HEADS // G
STACKED = ((0, 0, 1, 1, 0, 2), (0, 1, 0, 1, 2, 0))
STACK = len(STACKED[0]) * HD
LEAD = 8
SOFTMAX_SCALE = 0.25
RMS_EPS, LN_EPS = 1e-6, 1e-5
DELTA_SCALE = 0.1
ROUND = 1.5 * 2.0 ** 23
HYPER = 2 * BN * D // 2
SLICE = HYPER // B
HN = 256

STAGGER = 1
UNROLL = 4

AG, AB, FG, FB, L1S = range(5)
NV = 5
R_ALPHA_A, R_ALPHA_F, R_ALPHA_F_B, R_L3 = range(4)
NR = 4


END = object()


class Mark:

    def __init__(self, counter, section, at):
        self.counter, self.section, self.at = counter, section, at


class Counter:

    def __init__(self, prog, sem, step):
        self.prog, self.sem, self.step, self.n, self.pre = prog, sem, step, 0, 0

    def mark(self):
        self.n += self.step
        return Mark(self, self.prog.section, self.n)


class Slot:

    def __init__(self, prog, name):
        self.name, self.free = name, []
        prog.slots.append(self)


class Section:
    def __init__(self, trips):
        self.trips, self.items, self.before, self.start, self.total, self.left = (
            trips, {}, {}, {}, {}, {})


class Engine:
    def __init__(self, prog, name, sem):
        self.prog, self.name = prog, name
        self.counter = Counter(prog, sem, 1)
        self.carrier = prog.carrier if name in ("pool", "sp") else None

    def __call__(self, fn, after=(), mark=None, carried=False):
        item = [fn, list(after), None, carried]
        self.prog.section.items.setdefault(self.name, []).append(item)
        self.last = item
        if mark is not None:
            item[2] = mark
            return mark.mark()
        return None

    def mark(self):
        if self.last[2] is None:
            self.last[2] = self.counter
            return self.counter.mark()
        return Mark(self.last[2], self.prog.section, self.last[2].n)

    def wait(self, *marks):
        self.prog.section.items.setdefault(self.name, []).append([None, list(marks), None, True])

    def play(self, e):
        for c in [self.counter] + [c for c in self.prog.counters if c.step != 1 and self.name == "sp"]:
            if c.pre:
                e.sem_inc(c.sem, c.pre)
        for section in self.prog.sections:
            items = section.items.get(self.name, [])
            if section.trips:
                for c, n in section.start.items():
                    if n:
                        e.wait_ge(c.sem, c.pre + n)
                if items:
                    with e.Fori(0, section.trips) as i:
                        self.play_items(e, items, section, i)
            else:
                self.play_items(e, items, section, None)

    def play_items(self, e, items, section, i):
        seen = {}
        for fn, marks, raised, carried in items:
            need = {}
            for m, back in [(m, 0) for m in marks if isinstance(m, Mark)] + [
                (m, 1) for s in marks if isinstance(s, str) for m in section.left.get(s, [])
            ]:
                c = m.counter
                if section.trips and m.section is not section:
                    continue
                at = m.at
                if m.section is not section and m.section.trips:
                    at += (m.section.trips - 1) * m.section.total[c]
                if back:
                    at -= section.total[c]
                need[c] = max(need.get(c, at), at)
            for c, at in need.items():
                if at <= seen.get(c, -(10 ** 9)):
                    continue
                seen[c] = at
                e.wait_ge(c.sem, i * section.total[c] + (c.pre + at) if section.trips else c.pre + at)
                if section.trips and (self.carrier is not None or carried):
                    e.sem_inc(self.prog.carrier, 1)
            if fn is not None:
                ins = fn(e, i)
                if raised is not None:
                    ins.then_inc(raised.sem, raised.step)


class Program:

    def __init__(self, nc, ctx):
        self.nc, self.ctx = nc, ctx
        self.slots, self.counters = [], []
        self.carrier = ctx.enter_context(nc.semaphore("carrier"))
        self.sections = [Section(0)]
        self.section = self.sections[0]

    def sem(self, name):
        return self.ctx.enter_context(self.nc.semaphore(name))

    def engine(self, name):
        e = Engine(self, name, self.sem(f"done_{name}"))
        self.counters.append(e.counter)
        return e

    def dma_counter(self, name):
        c = Counter(self, self.sem(f"dma_{name}"), 16)
        self.counters.append(c)
        return c

    def slot(self, name):
        return Slot(self, name)

    def loop(self, trips, own=()):
        s = Section(trips)
        s.before = {c: c.n for c in self.counters}
        s.start = {c: c.n for c in self.counters if c not in own}
        self.sections.append(s)
        self.section = s
        for slot in self.slots:
            slot.free = [slot.name]

    def end_loop(self):
        s = self.section
        for c in self.counters:
            s.total[c] = c.n - s.before[c]
            c.n = s.before[c] + s.trips * s.total[c]
            c.pre = max(c.pre, s.total[c])
        for slot in self.slots:
            s.left[slot.name] = [m for m in slot.free if isinstance(m, Mark)]
        self.sections.append(Section(0))
        self.section = self.sections[-1]
        for slot in self.slots:
            slot.free = s.left[slot.name]


def weave(*flows):
    live = [[f[0], f[1], f[2] if len(f) > 2 else 10 ** 6] for f in flows]
    while live:
        for f in list(live):
            for _ in range(f[1]):
                if next(f[0], END) is END:
                    f[2] = 0
                    break
            f[2] -= 1
            if f[2] <= 0:
                live.remove(f)


def take(flow, n):
    for _ in range(n):
        next(flow, None)


def run(flow):
    for _ in flow:
        pass


def cond_seq(nc, x, cond_t, vec_t, row_t, wqk_t, wv_t, wo_t, wg_t, wh_t, wout_t, out_b, wup_t, wdown_t,
             hyper, wd_t, bdd_t, wu_t, bdu_t, bd, bu, lin_b, ln_w, ln_b, out):
    with ExitStack() as ctx:
        prog = Program(nc, ctx)
        pe, act, dve, pool, sp = (prog.engine(n) for n in ("pe", "act", "dve", "pool", "sp"))

        def dram(name, shape, dt):
            return nc.dram_tensor(name, shape, dt, kind="Internal").ap()

        qk_dram = dram("qk_parts", (2, 3, D, T), BF16)
        rows_dram = dram("rows", (B, NR * D), F32)
        hyper_dram = dram("hyper_out", (2 * B, HYPER), F32)
        mid_dram = dram("mid", (B, P, TT, D), F32)

        def sb(name, shape, dt=F32, on=ctx):
            return on.enter_context(nc.sbuf_tensor(name, shape, dt))

        psum = ctx.enter_context(nc.psum_tensor("psum", [P, 8, 512], F32))
        bank = [prog.slot(f"bank{k}") for k in range(8)]

        def mm(out_, lhs, rhs, start, stop, after=(), **kw):
            pe(lambda e, i: e.matmul(out_, lhs, rhs, start=start, stop=stop, **kw), after)

        def transpose(out_, in_, ident_, after=()):
            pe(lambda e, i: e.transpose(out_, in_, ident_), after)

        def activation(out_, in_, func, after=(), **kw):
            act(lambda e, i: e.activation(out_, in_, func, **kw), after)
            return act.mark()

        def copy(eng, out_, in_, after=()):
            if eng is act:
                return activation(out_, in_, ACT.Copy, after)
            eng(lambda e, i: e.tensor_copy(out_, in_), after)
            return eng.mark()

        def tt(eng, out_, a, b, op, after=()):
            eng(lambda e, i: e.tensor_tensor(out_, a, b, op), after)
            return eng.mark()

        def ts(eng, out_, a, s1, s2, op0, op1, after=()):
            eng(lambda e, i: e.tensor_scalar(out_, a, s1, s2, op0, op1), after)
            return eng.mark()

        def dma(counter, dst, src, after=()):
            def start(e, i):
                return e.dma_start(dst(i) if callable(dst) else dst, src(i) if callable(src) else src)
            return sp(start, after, mark=counter)

        def f32(ap):
            return ap.bitcast(F32)

        def fp32_terms(high, low, w_high, w_low):
            return ((high, w_high), (high, w_low), (low, w_high))

        ident = sb("ident", [P, P])
        ident16 = sb("ident16", [P, P], BF16)
        ones = sb("ones", [P, P])
        mhalf = sb("mhalf", [P, TT])
        zero = sb("zero", [P, 1])
        spare = sb("spare", [P, 1])
        rounds = sb("rounds", [P, 2])
        vecs = sb("vecs", [P, NV * KC, B])
        vec = sb("vec", [P, NV * KC])
        hyper_lhs = sb("hyper_lhs", [P, 32])
        down_mean = sb("down_mean", [P, 1])
        bc = sb("bc", [P, 3, D])

        wbase = sb("wbase", [P, 2, D])
        bd_col = sb("bd_col", [P, 1])
        bu_bc = sb("bu_bc", [P, D])
        w2_bc = sb("w2_bc", [P, D])

        pool(lambda e, i: e.memset(ident[:, :], 0.0))
        m = pool.mark()
        pool(lambda e, i: e.affine_select(out=ident[:, :], in_=ident[:, :], compare_op=ALU.not_equal, fill=1.0,
                                          base=0, pattern=[[-1, P]], channel_multiplier=1), [m])
        m = pool.mark()
        copy(pool, ident16[:, :], ident[:, :], [m])
        pool(lambda e, i: e.memset(ones[:, :], 1.0))
        pool(lambda e, i: e.memset(mhalf[:, :], -0.5))
        pool(lambda e, i: e.memset(zero[:, :], 0.0))
        pool(lambda e, i: e.memset(rounds[:, 0:1], ROUND))
        pool(lambda e, i: e.memset(rounds[:, 1:2], -ROUND))
        pool(lambda e, i: e.memset(hyper_lhs[:, :], 0.0))
        const = pool.mark()

        big = ExitStack()
        QS = sb("QS", [P, HEADS, T], BF16, big)
        KS = sb("KS", [P, HEADS, T], BF16, big)
        Hh = sb("Hh", [P, KC, T], F32R, big)
        Hl = sb("Hl", [P, KC, T], F32R, big)
        H = sb("H", [P, KC * T], F32, big)
        XN = H[:, :].rearrange("p (t d) -> p t d", t=TT)
        XA = sb("XA", [P, TT, D], F32, big)
        X1 = sb("X1", [P, TT, D], F32, big)
        VA = sb("VA", [P, TT, HEADS, 2 * HD], F32, big)
        MR = sb("MR", [3 * G, T], BF16, big)
        NM = sb("NM", [P, NG, TT, G], F32, big)
        NMp = sb("NMp", [P, TT, 3, G], BF16, big)
        NMr = sb("NMr", [P, TT, G], F32, big)
        ss = sb("ss", [P, TT], F32, big)
        rms = sb("rms", [P, 2, TT], F32, big)
        rec = sb("rec", [P, TT, G], F32, big)
        quant = sb("quant", [P, 2, 6], F32, big)
        HW = sb("HW", [P, G * HN], F32, big)
        HO = sb("HO", [P, HN], F32, big)
        def split_pair(name, chunks, n):
            high = sb(name + "_high", [P, chunks, n], F32R, big)
            with ExitStack() as s:
                whole = sb(name + "_whole", [P, chunks, n], F32, s)
            return high, sb(name + "_low", [P, chunks, n], F32R, big), whole

        WQKh, WQKl, WQK = split_pair("WQK", KC, 2 * D)
        WVh, WVl, WV = split_pair("WV", KC, D)
        WOh, WOl, WO = split_pair("WO", KC, D)
        WGh, WGl, WG = split_pair("WG", KC, FF)
        WHh, WHl, WH = split_pair("WH", KC, FF)
        WOUTh, WOUTl, WOUT = split_pair("WOUT", FC, D)
        WUPh, WUPl, WUP = split_pair("WUP", KC, 2 * FF)
        WDN = sb("WDN", [P, FC, D], BF16, big)

        base = nc.sbuf_base
        with ExitStack() as s:
            PR = sb("PR", [P, 2, G, T], F32, s)
        with ExitStack() as s:
            Gh = sb("Gh", [P, KC, T], F32R, s)
            Gl = sb("Gl", [P, KC, T], F32R, s)
            QT = sb("QT", [P, 2, 3, T], BF16, s)
            QR = sb("QR", [P, T], F32, s)
        with ExitStack() as s:
            ROWV = sb("ROWV", [P, 4 * D], F32, s)
        with ExitStack() as s:
            HV = sb("HV", [P, 2, FF], F32, s)
            Q16 = sb("Q16", [P, 2, FF], BF16, s)
            QT16 = sb("QT16", [P, 2, FC, P], BF16, s)
        sb("hold_first", [P, 2 * G * T], F32, big)
        with ExitStack() as s:
            OA = sb("OA", [P, 2, T], F32, s)
            ON = sb("ON", [P, TT, D], F32, s)
            OTh = sb("OTh", [P, KC, T], F32R, s)
            OTl = sb("OTl", [P, KC, T], F32R, s)
        with ExitStack() as s:
            TAB = sb("TAB", [P, (NV + 3) * D], F32, s)
            DW = sb("DW", [P, FC * D], F32, s)
        with ExitStack() as s:
            SG = sb("SG", [P, 2, T], F32, s)
            PP = sb("PP", [P, 2, T], F32, s)
            PPh = sb("PPh", [P, 2, T], F32R, s)
            PPl = sb("PPl", [P, 2, T], F32R, s)
        sb("hold_second", [P, 8 * T], F32, big)

        slot = {n: prog.slot(n) for n in
                ("QS", "KS", "H0", "H1", "Hparts", "Gparts", "QR", "XA", "X1", "VA", "MR", "NMp",
                 "ss0", "ss1", "rms0", "rms1", "vec", "bc",
                 "HW", "HO", "QT0", "QT1", "PR0", "PR1", "HV0", "HV1", "Q160", "Q161", "QT160", "QT161",
                 "OA0", "OA1", "ON", "OT", "SG0", "SG1", "PP0", "PP1", "PX0", "PX1", "quant0", "quant1",
                 "qk_dram0", "qk_dram1")}
        c_in, c_rowv, c_x, c_res, c_bc, c_hw, c_ho, c_m, c_mid = (
            prog.dma_counter(n) for n in ("in", "row_vectors", "x", "residual", "rows", "hyper", "hyper_out", "maxima", "mid"))
        c_w = {n: prog.dma_counter("w_" + n) for n in ("qk", "v", "o", "gate", "hidden", "out", "up", "down", "l2")}
        c_qk = [prog.dma_counter(f"qk_out{k}") for k in range(2)]
        c_stack = [prog.dma_counter(f"stacks{k}") for k in range(2)]

        cond2 = HO[:, 0:B]
        dma(c_in, cond2[0:NC, :], cond_t)
        dma(c_in, cond2[NC:P, :], cond_t)
        dma(c_in, TAB[0:NC, 0:NV * D], vec_t)
        tables_in = dma(c_in, TAB[0:NC, NV * D:(NV + 3) * D], row_t)
        slot["XA_ready"] = dma(c_x, XA[:, :, :], x[0].rearrange("(t p) d -> p t d", p=P))

        def load_weights(name, whole, src, queue=sp):
            src = src.rearrange("(c p) n -> p c n", p=P)
            return queue(lambda e, i: e.dma_start(whole, src), mark=c_w[name])

        arrived = {"qk": load_weights("qk", WQK[:, :, :], wqk_t), "v": load_weights("v", WV[:, :, :], wv_t)}
        for n, v in enumerate((lin_b, ln_w, ln_b, out_b)):
            rowv_in = dma(c_rowv, ROWV[0:B, n * D:(n + 1) * D], v.partition_broadcast(B))

        def split_weights(name, high, low, whole, there, eng=dve):
            h2, l2, w2 = (w[:, :, :].rearrange("p c n -> p (c n)") for w in (high, low, whole))
            m_high = copy(act, h2, w2, [there])
            return tt(eng, l2, w2, f32(h2), ALU.subtract, [m_high])

        for t in range(TT):
            pool(lambda e, i, t=t: e.memset(VA[:, t, :, HD:2 * HD], 1.0))
        va_init = pool.mark()
        dve(lambda e, i: e.memset(KS[STACK:STACK + 3, :, :], 1.0))
        ones_there = dve.mark()

        copy(dve, hyper_lhs[0:NC, 0:B], cond2[0:NC, :], [tables_in, const])
        hyper_ready = copy(dve, hyper_lhs[NC:P, B:2 * B], cond2[NC:P, :])
        for v in range(NV * KC):
            mm(psum[:, 0, v * B:(v + 1) * B], TAB[0:NC, v * P:(v + 1) * P], cond2[0:NC, :], True, True, [tables_in])
        m_vec = pe.mark()
        for k in range(2):
            n = min(512, 3 * D - 512 * k)
            mm(psum[0:B, 6 + k, 0:n], cond2[0:NC, :], TAB[0:NC, NV * D + 512 * k:NV * D + 512 * k + n], True, True)
        m_tab = pe.mark()
        m_v = copy(dve, vecs[:, :, :].rearrange("p v b -> p (v b)"), psum[:, 0, 0:NV * KC * B], [m_vec])
        m_v = ts(dve, vecs[:, L1S * KC:(L1S + 1) * KC, :], vecs[:, L1S * KC:(L1S + 1) * KC, :], 1.0, None,
                 ALU.add, ALU.bypass, [m_v])
        slot["vec"].free = [m_v]
        slot["VA"].free = [va_init]
        bank[0].free = [m_v]
        slot["HO"].free = [m_tab, hyper_ready]

        def norm(th, src, src_ready, gamma, beta, banks, to="H", high_by=None):
            high_by = high_by or act
            high, low = {"H": (Hh, Hl), "G": (Gh, Gl)}[to]
            last = th == TT // 2 - 1
            tiles = (2 * th, 2 * th + 1)
            two = slice(2 * th, 2 * th + 2)
            tokens = slice(2 * th * P, (2 * th + 2) * P)
            for t in tiles:
                dve(lambda e, i, t=t: e.tensor_tensor_reduce(
                    out=XN[:, t, :], in0=src[:, t, :], in1=src[:, t, :], scale=1.0, scalar=0.0,
                    op0=ALU.mult, op1=ALU.add, accum_out=ss[:, t:t + 1]),
                    src_ready[t] + slot[f"H{th}"].free + slot[f"ss{th}"].free)
            m = ts(pool, rms[:, 0, two], ss[:, two], 1.0 / D, RMS_EPS, ALU.mult, ALU.add,
                   [dve.mark()] + slot[f"rms{th}"].free)
            slot[f"ss{th}"].free = [m]
            m = tt(pool, rms[:, 1, two], rms[:, 0, two], mhalf[:, two], ALU.pow, [m])
            yield
            for t in tiles:
                ts(dve, XN[:, t, :], src[:, t, :], rms[:, 1, t:t + 1], None, ALU.mult, ALU.bypass, [m])
            m = dve.mark()
            slot[f"rms{th}"].free = [m]
            yield
            for c in range(KC):
                for t2, t in enumerate(tiles):
                    transpose(psum[:, banks[c], t2 * P:(t2 + 1) * P], XN[:, t, c * P:(c + 1) * P], ident[:, :],
                              [m] + bank[banks[c]].free)
            up = pe.mark()
            yield
            whole = XN[:, two, :].rearrange("p t d -> p (t d)").rearrange("p (c n) -> p c n", c=KC)
            mh, mw = {}, {}
            for ca in range(KC):
                for c, part in ((ca, "high"), (KC - 1 - ca, "whole")):
                    g = vec[:, gamma * KC + c:gamma * KC + c + 1]
                    b = vec[:, beta * KC + c:beta * KC + c + 1] if beta is not None else None
                    seen = psum[:, banks[c], 0:2 * P]
                    if part == "high" and high_by is dve:
                        mh[c] = ts(dve, high[:, c, tokens], seen, g, b, ALU.mult, ALU.bypass if b is None else ALU.add,
                                   [up] + slot[to + "parts"].free)
                    elif part == "high":
                        mh[c] = activation(high[:, c, tokens], seen, ACT.Identity, [up] + slot[to + "parts"].free
                                           + ([mw[c]] if ca else []), scale=g, bias=zero[:, :] if b is None else b)
                    else:
                        mw[c] = ts(dve, whole[:, c, :], seen, g, b, ALU.mult, ALU.bypass if b is None else ALU.add,
                                   [up] + ([mh[c]] if ca and high_by is act else []))
            slot["H_high"][th] = [mh[KC - 1]]
            for c in range(KC):
                bank[banks[c]].free = [mh[c], mw[c]]
            yield
            ml = tt(dve, low[:, :, tokens], whole, f32(high[:, :, tokens]), ALU.subtract,
                    [mh[KC - 1], mw[0]] + slot[to + "parts"].free)
            slot[f"H{th}"].free = [ml]
            for t in tiles:
                slot["H_tile"][t] = [ml]
            if last:
                slot["vec_read"] = [mh[KC - 1], mw[0]]
            yield

        def load_vec(index, after):
            dve(lambda e, i: e.tensor_copy(vec[:, :], vecs[:, :, bass.ds(index(i), 1)].rearrange("p v o -> p (v o)")),
                after)
            return dve.mark()

        def next_batch(i):
            return 0 if i is None else (i + 1) % B

        def load_next():
            slot["XA_ready"] = dma(c_x, XA[:, :, :], lambda i: x[bass.ds(next_batch(i), 1)].rearrange("o (t p) d -> p (o t) d", p=P)
                        if i is not None else x[0].rearrange("(t p) d -> p t d", p=P), slot["XA"].free)

        def norm_next(high_by):
            mv = load_vec(next_batch, slot["vec"].free)
            if high_by is act:
                act.wait(mv)
            halves = [norm(th, XA, [[slot["XA_ready"]]] * TT, AG, AB, (2 * th, 2 * th + 1), high_by=high_by)
                      for th in range(2)]
            for turn in range(5):
                next(halves[0])
                if turn == 3:
                    yield
                next(halves[1])
                if turn == 1:
                    slot["XA"].free = [dve.mark()]
                yield
            slot["H_next"] = slot["H_tile"][TT - 1]
            slot["vec"].free = slot["vec_read"]

        def qk_next(half, banks):
            done = []
            slot["QT_out"] = []
            for wq in range(2):
                bk = banks[wq]
                cols = slice((wq * KC + half) * P, (wq * KC + half + 1) * P)
                k = 0
                for kc in range(KC):
                    for w, h in ((WQKh, Hh), (WQKh, Hl), (WQKl, Hh)):
                        mm(psum[:, bk, :], w[:, kc, cols], h[:, kc, :], k == 0, k == 5,
                           slot["H_next"] + bank[bk].free if k == 0 else ())
                        k += 1
                done += [pe.mark()]
                slot["Hparts"].free = done[-1:]
                yield
            for wq in range(2):
                bk = banks[wq]
                qt = slot[f"QT{wq}"]
                m = activation(QT[:, wq, 0, :], psum[:, bk, :], ACT.Copy, done[wq:wq + 1] + qt.free)
                m = tt(dve, QR[:, :], psum[:, bk, :], QT[:, wq, 0, :], ALU.subtract, [m] + slot["QR"].free)
                bank[bk].free = [m]
                m = activation(QT[:, wq, 1, :], QR[:, :], ACT.Copy, [m])
                if wq == 1:
                    yield
                ml = tt(dve, QT[:, wq, 2, :], QR[:, :], QT[:, wq, 1, :], ALU.subtract, [m])
                slot["QR"].free = [ml]
                w = dma(c_qk[wq], qk_dram[wq, :, half * P:(half + 1) * P, :].rearrange("h p t -> p h t"), QT[:, wq, :, :],
                        [ml] + slot[f"qk_dram{half}"].free)
                qt.free = [w]
                S, name = ((QS, "QS"), (KS, "KS"))[wq]
                for row, part in enumerate(STACKED[wq]):
                    src = qk_dram[wq, part, half * P:(half + 1) * P, :].rearrange("(h r) t -> r h t", r=HD)
                    loaded = dma(c_stack[half], S[row * HD:(row + 1) * HD, 8 * half:8 * half + 8, :], src,
                                 [w] + slot[name].free)
                if wq == 0:
                    yield
                slot["QT_out"].append(w)
            slot[f"qk_dram{half}"].free = [loaded]
            slot[f"stacks{half}"] = [loaded]
            yield

        def v_next(banks):
            done = []
            for th in range(TT // 2):
                bk = banks[th]
                for t2 in range(2):
                    t = 2 * th + t2
                    k = 0
                    for kc in range(KC):
                        for h, w in fp32_terms(Hh, Hl, WVh, WVl):
                            mm(psum[:, bk, t2 * D:(t2 + 1) * D], h[:, kc, t * P:(t + 1) * P], w[:, kc, :], k == 0, k == 5,
                               slot["H_next"] + bank[bk].free if k == 0 and t2 == 0 else ())
                            k += 1
                done += [pe.mark()]
                slot["Hparts"].free = done[-1:]
                yield
            for th in range(TT // 2):
                m2 = copy(act, VA[:, 2 * th:2 * th + 2, :, 0:HD],
                          psum[:, banks[th], :].rearrange("p (t h d) -> p t h d", t=2, h=HEADS), [done[th]] + slot["VA"].free)
                bank[banks[th]].free = [m2]
            slot["V_ready"] = [m2]

        started = [False]

        RING = (4, 5, 6)
        ring_at = [0]

        def ring():
            k = RING[ring_at[0] % len(RING)]
            ring_at[0] += 1
            return k

        def maxima(h, t, k, tiles=2):
            free = [m for b in range(tiles) for m in bank[k + b].free]
            for b in range(tiles):
                mm(psum[:, k + b, :], QS[0:STACK, h, (t + b) * P:(t + b + 1) * P], KS[0:STACK, h, :], True, True,
                   ([f"stacks{h // 8}"] if started[0] else slot[f"stacks{h // 8}"]) + free)
            m = pe.mark()
            out_ = NM[:, h // G, t:t + tiles, h % G]
            dve(lambda e, i: e.tensor_reduce(out_, psum[:, k:k + tiles, :], AX.X, ALU.max, negate=True), [m])
            r = dve.mark()
            for b in range(tiles):
                bank[k + b].free = [r]
            slot["nm"] = r

        def maxima_parts(g):
            m = copy(dve, NMp[:, :, 0, :], NM[:, g, :, :], [slot["nm"]] + slot["NMp"].free)
            yield
            m = tt(dve, NMr[:, :, :], NM[:, g, :, :], NMp[:, :, 0, :], ALU.subtract, [m])
            yield
            m = copy(dve, NMp[:, :, 1, :], NMr[:, :, :], [m])
            yield
            slot["parts"] = tt(dve, NMp[:, :, 2, :], NMr[:, :, :], NMp[:, :, 1, :], ALU.subtract, [m])
            yield

        def maxima_rows(g, k):
            rows = psum[0:3 * G, k, :].bitcast(BF16)[:, 0:T]
            for t in range(TT):
                transpose(rows[:, t * P:(t + 1) * P], NMp[:, t, :, :].rearrange("p q j -> p (q j)"), ident16[:, :],
                          [slot["parts"]] + bank[k].free)
            m = pe.mark()
            slot["NMp"].free = [m]
            m = activation(MR[:, :], rows, ACT.Copy, [m] + slot["MR"].free)
            bank[k].free = [m]
            for part in range(3):
                r = STACK + part
                dma(c_m, QS[r:r + 1, G * g:G * g + G, :], MR[G * part:G * part + G, :], [m])
            slot["mrow"][g] = [Mark(c_m, prog.section, c_m.n)]
            slot["MR"].free = slot["mrow"][g]

        def maxima_lead(banks):
            started[0] = False
            parts = iter(())
            for h in range(LEAD):
                for t in range(TT):
                    maxima(h, t, banks[(h * TT + t) % len(banks)], 1)
                    if t < TT - 1 or h % G:
                        next(parts, None)
                    if h >= G and h % G == 1 and t == 1:
                        maxima_rows(h // G - 1, banks[(h * TT + t + 1) % len(banks)])
                    yield
                if h % G == G - 1:
                    parts = maxima_parts(h // G)
            run(parts)
            yield
            maxima_rows(LEAD // G - 1, banks[0])
            yield

        def attention():
            started[0] = True
            slot["mrow"] = {g: [f"mrow{g}"] for g in range(LEAD // G)}

            def products(g, kc, pr, ready):
                for j in range(G):
                    mm(psum[32 * j:32 * j + 32, 7, :], VA[:, kc, G * g + j, :], PR[:, pr, j, :], kc == 0, kc == TT - 1,
                       ready + (bank[7].free if kc == 0 else []) + ["V_ready"], tile_position=(0, 32 * j))
                m = pe.mark()
                slot[f"PR{pr}"].free = [m]
                return m

            def group_out(g, m):
                b = g % 2
                m = copy(act if g < 1 else dve, OA[:, b, :], psum[:, 7, :], [m] + slot[f"OA{b}"].free)
                bank[7].free = [m]
                return m

            def group_norm(g, m, k):
                b = g % 2
                for t in range(TT):
                    transpose(psum[:, k, t * P:(t + 1) * P], OA[:, b, t * P:(t + 1) * P], ident[:, :],
                              [m] + bank[k].free)
                m = pe.mark()
                slot[f"OA{b}"].free = [m]
                o = psum[:, k, :].rearrange("p (t j d) -> p t j d", t=TT, j=G)
                dve(lambda e, i: e.reciprocal(rec[:, :, :], o[:, :, :, HD]), [m])
                m = dve.mark()
                dst = ON[:, :, g * G * HD:(g + 1) * G * HD].rearrange("p t (j d) -> p t j d", j=G)
                r4 = rec[:, :, :].unsqueeze(3).broadcast_to([P, TT, G, HD])
                m = tt(dve, dst, o[:, :, :, 0:HD], r4, ALU.mult, [m] + (slot["ON"].free if g == 0 else []))
                bank[k].free = [m]
                return m

            def scores(h, kc, pr, j):
                k = ring()
                mm(psum[:, k, :], KS[0:STACK + 3, h, kc * P:(kc + 1) * P], QS[0:STACK + 3, h, :], True, True,
                   [f"stacks{h // 8}"] + slot["mrow"][h // G] + bank[k].free)
                m = pe.mark()
                m = activation(PR[:, pr, j, :], psum[:, k, :], ACT.Exp, [m] + slot[f"PR{pr}"].free, scale=SOFTMAX_SCALE)
                bank[k].free = [m]
                return m

            pend, evac, parts = None, None, None
            for step in range(HEADS):
                g, kc = divmod(step, G)
                pr = kc % 2
                lead = step + LEAD
                scores(G * g, kc, pr, 0)
                scores(G * g + 1, kc, pr, 1)
                if lead < HEADS:
                    maxima(lead, 0, 0)
                scores(G * g + 2, kc, pr, 2)
                if evac is not None:
                    group_norm(*evac, 2 if step < LEAD + 2 else 0)
                    evac = None
                if pend is not None:
                    m = products(*pend)
                    if pend[1] == TT - 1:
                        evac = (pend[0], group_out(pend[0], m))
                done = scores(G * g + 3, kc, pr, 3)
                if parts is not None:
                    maxima_rows(parts, ring())
                    parts = None
                if lead < HEADS:
                    maxima(lead, 2, 2)
                    if lead % G == G - 1:
                        parts = lead // G
                        run(maxima_parts(parts))
                pend = (g, kc, pr, [done])
                yield
            m = products(*pend)
            slot["VA"].free = slot["KS"].free = slot["QS"].free = [m]
            mo = group_out(pend[0], m)
            yield
            slot["ON_ready"] = [group_norm(pend[0], mo, 6)]
            yield

        def attn_out(tb, ob):
            for c in range(KC):
                for t in range(TT):
                    transpose(psum[:, tb[c], t * P:(t + 1) * P], ON[:, t, c * P:(c + 1) * P], ident[:, :],
                              slot["ON_ready"] + bank[tb[c]].free)
                m = pe.mark()
                mh = activation(OTh[:, c, :], psum[:, tb[c], :], ACT.Copy, [m] + slot["OT"].free)
                ml = tt(dve, OTl[:, c, :], psum[:, tb[c], :], f32(OTh[:, c, :]), ALU.subtract, [mh])
                bank[tb[c]].free = [ml]
            slot["ON"].free = [m]
            yield
            done = []
            for th in range(2):
                bk = ob[th]
                for t2 in range(2):
                    t = 2 * th + t2
                    k = 0
                    for kc in range(KC):
                        for h, w in fp32_terms(OTh, OTl, WOh, WOl):
                            mm(psum[:, bk, t2 * D:(t2 + 1) * D], h[:, kc, t * P:(t + 1) * P], w[:, kc, :], k == 0, k == 5,
                               [ml] + (bank[bk].free if t2 == 0 else []) if k == 0 else ())
                            k += 1
                done += [pe.mark()]
            slot["OT"].free = done[1:]
            yield
            for th in range(2):
                al = bc[:, R_ALPHA_A:R_ALPHA_A + 1, :].broadcast_to([P, 2, D])
                dst = ON[:, 2 * th:2 * th + 2, :]
                m2 = tt(dve, dst, psum[:, ob[th], :].rearrange("p (t d) -> p t d", t=2), al, ALU.mult,
                        [done[th]] + slot["ON"].free + slot["bc_ready"])
                bank[ob[th]].free = [m2]
                x1 = X1[:, 2 * th:2 * th + 2, :]
                m2 = tt(dve, x1, x1, dst, ALU.add, [m2] + slot["X1_ready"])
                slot["X1_tile"][2 * th] = slot["X1_tile"][2 * th + 1] = [m2]
                if th:
                    slot["ON"].free = [m2]
                yield

        def swiglu():
            pend = None

            def out_products(f, b, ready_):
                for t in range(TT):
                    bk = 4 + t // 2
                    k = 0
                    for h, w in fp32_terms(PPh, PPl, WOUTh, WOUTl):
                        mm(psum[:, bk, (t % 2) * D:(t % 2 + 1) * D], h[:, b, t * P:(t + 1) * P], w[:, f, :],
                           f == 0 and k == 0 and t % 2 == 0, f == FC - 1 and k == 2, ready_ + (bank[bk].free if f == 0 else []),
                           skip_group_check=True)
                        k += 1
                    if t % 2:
                        slot[f"PX{b}"].free = [pe.mark()]
                        slot["halves"][t // 2] = pe.mark()
                        yield

            for f in range(FC):
                b = f % 2
                gb, hb = 2 * b, 2 * b + 1
                cols = slice(f * P, (f + 1) * P)
                marks = []
                pair = (((WGh, WGl), gb), ((WHh, WHl), hb))
                for n in range(2 if f == 0 else 1):
                    tok = slice(n * T // 2, (n + 1) * T // 2) if f == 0 else slice(0, T)
                    high, low = ([m[n], m[1]][f > 0] for m in (slot["H_high"], slot["H_tile"][1:3]))
                    for (wh, wl), bk in pair:
                        for kc in range(KC):
                            for w in (wh, wl):
                                mm(psum[:, bk, tok], w[:, kc, cols], Gh[:, kc, tok], kc == 0 and w is wh, False,
                                   high + bank[bk].free)
                    if f:
                        yield
                    for (wh, wl), bk in pair:
                        for kc in range(KC):
                            mm(psum[:, bk, tok], wh[:, kc, cols], Gl[:, kc, tok], False, kc == KC - 1, low)
                        marks.append(pe.mark())
                    if f == 0 and n == 0:
                        yield
                marks = marks[-2:]
                m = activation(SG[:, b, :], psum[:, gb, :], ACT.Silu, [marks[0]] + slot[f"SG{b}"].free)
                bank[gb].free = [m]
                m = tt(dve, PP[:, b, :], SG[:, b, :], psum[:, hb, :], ALU.mult, [m, marks[1]] + slot[f"PP{b}"].free)
                bank[hb].free = [m]
                slot[f"SG{b}"].free = [m]
                mh = activation(PPh[:, b, :], PP[:, b, :], ACT.Copy, [m] + slot[f"PX{b}"].free)
                yield
                ml = tt(dve, PPl[:, b, :], PP[:, b, :], f32(PPh[:, b, :]), ALU.subtract, [mh])
                slot[f"PP{b}"].free = [ml]
                if pend is not None:
                    yield from out_products(*pend)
                pend = (f, b, [ml])
            slot["Gparts"].free = [marks[1]]
            last = out_products(*pend)
            run(last)
            yield
            for th in range(2):
                m = slot["halves"][th]
                al = bc[:, R_ALPHA_F:R_ALPHA_F + 1, :].broadcast_to([P, 2, D])
                dst = PP[:, th, :].rearrange("p (t d) -> p t d", t=2)
                m2 = tt(dve, dst, psum[:, 4 + th, :].rearrange("p (t d) -> p t d", t=2), al, ALU.mult,
                        [m] + slot[f"PP{th}"].free)
                bank[4 + th].free = [m2]
                x1 = X1[:, 2 * th:2 * th + 2, :]
                m2 = tt(dve, x1, x1, dst, ALU.add, [m2] + slot["X1_ready"])
                slot[f"PP{th}"].free = [m2]
                slot["X1_tile"][2 * th] = slot["X1_tile"][2 * th + 1] = [m2]
                yield
            slot["bc"].free = [m2]

        def geglu():
            pend = None

            def down(t, b, ready_):
                tb = psum[:, 4, :].bitcast(BF16)
                for f in range(FC):
                    transpose(tb[:, f * P:(f + 1) * P], Q16[:, b, f * P:(f + 1) * P], ident16[:, :],
                              ready_ + bank[4].free)
                m = pe.mark()
                slot[f"Q16{b}"].free = [m]
                m = copy(act, QT16[:, b, :, :].rearrange("p f t -> p (f t)"), tb, [m] + slot[f"QT16{b}"].free + slot["QT_out"])
                bank[4].free = [m]
                return m

            def finish(t, b, ready_):
                for f in range(FC):
                    mm(psum[:, 5, 0:D], QT16[:, b, f, :], WDN[:, f, :], f == 0, f == FC - 1, ready_ + bank[5].free)
                m = pe.mark()
                slot[f"QT16{b}"].free = [m]
                dve(lambda e, i: e.scalar_tensor_tensor(out=X1[:, t, :], in0=psum[:, 5, 0:D], scalar=quant[:, b, 2:3],
                                                        in1=X1[:, t, :], op0=ALU.mult, op1=ALU.add), [m])
                m = dve.mark()
                bank[5].free = [m]
                slot[f"quant{b}"].free = [m]
                return m

            pair = 0
            last = older = None
            for t in range(TT):
                b = t % 2
                for hf in range(2):
                    gb, vb = 2 * (pair % 2), 2 * (pair % 2) + 1
                    pair += 1
                    marks = []
                    tok = slice(t * P, (t + 1) * P)
                    both = [(bk, slice(off + hf * 512, off + hf * 512 + 512)) for bk, off in ((gb, FF), (vb, 0))]
                    for bk, cols in both:
                        for kc in range(KC):
                            for w in (WUPh, WUPl):
                                mm(psum[:, bk, :], Hh[:, kc, tok], w[:, kc, cols], kc == 0 and w is WUPh, False,
                                   slot["H_high"][t // 2] + bank[bk].free)
                    for bk, cols in both:
                        for kc in range(KC):
                            mm(psum[:, bk, :], Hl[:, kc, tok], WUPh[:, kc, cols], False, kc == KC - 1, slot["H_tile"][t])
                        marks.append(pe.mark())
                    yield
                    hv = HV[:, b, hf * 512:(hf + 1) * 512]
                    m = activation(hv, psum[:, gb, :], ACT.Gelu, [marks[0]] + slot[f"HV{b}"].free)
                    bank[gb].free = [m]
                    m = tt(dve, hv, hv, psum[:, vb, :], ALU.mult, [m, marks[1]])
                    bank[vb].free = [m]
                    dve(lambda e, i, b=b, hf=hf, hv=hv: e.tensor_reduce(
                        quant[:, b, 4 + hf:5 + hf], hv, AX.X, ALU.max, apply_absolute_value=True),
                        [m] + slot[f"quant{b}"].free)
                    if hf == 0 and older is not None:
                        finish(*older)
                    if hf == 1 and last is not None:
                        older = (*last[0:2], [down(*last)])
                    if t == TT - 1 and hf == 1:
                        activation(spare[:, :], zero[:, :], ACT.Exp)
                    yield
                hv = HV[:, b, :]
                m = tt(dve, quant[:, b, 0:1], quant[:, b, 4:5], quant[:, b, 5:6], ALU.max, [dve.mark()])
                m = ts(dve, quant[:, b, 1:2], quant[:, b, 0:1], 1e-5, 1.0 / 127.0, ALU.max, ALU.mult, [m])
                ts(dve, quant[:, b, 2:3], quant[:, b, 1:2], down_mean[:, :], None, ALU.mult, ALU.bypass, [m])
                dve(lambda e, i, b=b: e.reciprocal(quant[:, b, 3:4], quant[:, b, 1:2]))
                m = dve.mark()
                m2 = []
                free = slot[f"Q16{b}"].free + slot["QT_out"][0:1 + b]
                cut = FF // 2 if t == TT - 1 else FF
                if cut < FF:
                    md = ts(dve, hv[:, cut:], hv[:, cut:], quant[:, b, 3:4], ROUND, ALU.mult, ALU.add, [m])
                    m2 = [ts(dve, Q16[:, b, cut:], hv[:, cut:], ROUND, None, ALU.subtract, ALU.bypass,
                             [md] + free)]
                m = activation(hv[:, 0:cut], hv[:, 0:cut], ACT.Identity, [m], scale=quant[:, b, 3:4], bias=rounds[:, 0:1])
                m = activation(Q16[:, b, 0:cut], hv[:, 0:cut], ACT.Identity, [m] + free,
                               scale=1.0, bias=rounds[:, 1:2])
                slot[f"HV{b}"].free = [m] + m2
                last = (t, b, [m] + m2)
            slot["Hparts"].free = [marks[1]]
            finish(*older)
            yield
            m = down(*last)
            yield
            m = finish(last[0], last[1], [m])
            there = dma(c_mid, lambda i: mid_dram[bass.ds(i, 1)].rearrange("o p t d -> (o p) t d"), X1[:, :, :], [m])
            slot["X1"].free = [there]
            yield

        def hyper_load(q):
            slot["HW_ready"] = [dma(c_hw, HW[:, :], lambda i: hyper[:, bass.ds(i * SLICE + q * G * HN, G * HN)],
                                    slot["HW"].free)]

        def hyper_slice(banks):
            quarters = SLICE // (G * HN)
            for q in range(quarters):
                bk = banks[q]
                for j in range(G):
                    mm(psum[32 * j:32 * j + 32, bk, 0:HN], hyper_lhs[:, :], HW[:, j * HN:(j + 1) * HN], True, True,
                       slot["HW_ready"] + bank[bk].free, tile_position=(0, 32 * j))
                m = pe.mark()
                slot["HW"].free = [m]
                if q + 1 < quarters:
                    hyper_load(q + 1)
                m = copy(act, HO[:, :], psum[:, bk, 0:HN], [m] + slot["HO"].free)
                bank[bk].free = [m]
                for j in range(G):
                    dma(c_ho, lambda i, q=q, j=j: hyper_dram[:, bass.ds(i * SLICE + (q * G + j) * HN, HN)],
                        HO[32 * j:32 * j + 2 * B, :], [m])
                slot["HO"].free = [Mark(c_ho, prog.section, c_ho.n)]
                yield

        slot["H_tile"] = [[] for _ in range(TT)]
        slot["X1_tile"] = [[] for _ in range(TT)]
        slot["mrow"], slot["halves"], slot["H_high"] = {}, {}, {}

        run(norm_next(act))
        pe.wait(split_weights("qk", WQKh, WQKl, WQK, arrived["qk"]))
        pe.wait(split_weights("v", WVh, WVl, WV, arrived["v"]))
        run(qk_next(0, (2, 3)))
        pool.wait(*slot["QT_out"])
        for name, whole, src in (("o", WO[:, :, :], wo_t), ("gate", WG[:, :, :], wg_t), ("hidden", WH[:, :, :], wh_t),
                                 ("out", WOUT[:, :, :], wout_t), ("up", WUP[:, :, :], wup_t),
                                 ("down", DW[:, :].rearrange("p (c n) -> p c n", c=FC), wdown_t)):
            arrived[name] = load_weights(name, whole, src, pool)
        wbias = HW[:, 0:2 * D].rearrange("p (w n) -> p w n", w=2)
        for dst, src in ((wbase[:, 0, :].rearrange("p (c n) -> p c n", c=KC), wd_t.rearrange("(c p) n -> p c n", p=P)),
                         (wbase[:, 1, :], wu_t),
                         (wbias[:, 0, :].rearrange("p (c n) -> p c n", c=KC), bdd_t.rearrange("(c p) n -> p c n", p=P)),
                         (wbias[:, 1, :], bdu_t), (bd_col[:, :], bd.rearrange("(p o) -> p o", o=1)),
                         (bu_bc[:, :], bu.partition_broadcast(P)), (w2_bc[:, :], ln_w.partition_broadcast(P))):
            arrived["l2"] = pool(lambda e, i, dst=dst, src=src: e.dma_start(dst, src), mark=c_w["l2"])
        run(qk_next(1, (2, 3)))
        run(v_next((4, 5)))

        rowv = ROWV[0:B, :]
        rows = X1[0:B, :, :].rearrange("p t d -> p (t d)")
        copy(dve, rows[:, 0:2 * D], psum[0:B, 6, 0:2 * D], [m_tab, rowv_in])
        tt(dve, rows[:, 2 * D:3 * D], psum[0:B, 6, D:2 * D], rowv[:, 3 * D:4 * D], ALU.mult)
        m_rows = tt(dve, rows[:, 3 * D:4 * D], psum[0:B, 7, 0:D], rowv[:, 0:D], ALU.add)
        bank[6].free = bank[7].free = [m_rows]
        m = activation(rows[:, 3 * D:4 * D], rows[:, 3 * D:4 * D], ACT.Tanh, [m_rows])
        m = tt(dve, rows[:, 3 * D:4 * D], rows[:, 3 * D:4 * D], rowv[:, 2 * D:3 * D], ALU.add, [m])
        m = tt(dve, rows[:, 3 * D:4 * D], rows[:, 3 * D:4 * D], rowv[:, D:2 * D], ALU.mult, [m])
        m = tt(dve, rows[:, 3 * D:4 * D], rows[:, 3 * D:4 * D], rowv[:, 2 * D:3 * D], ALU.add, [m])
        rows_there = dma(c_in, rows_dram, rows, [m])
        slot["X1"].free = [rows_there]
        sp.wait(rows_there)

        lead = maxima_lead(tuple(range(8)))
        pe.wait(ones_there, va_init)
        act.wait(m_rows)
        ready = []
        for name, high, low, whole in (("o", WOh, WOl, WO), ("gate", WGh, WGl, WG), ("hidden", WHh, WHl, WH),
                                       ("out", WOUTh, WOUTl, WOUT), ("up", WUPh, WUPl, WUP)):
            ready.append(split_weights(name, high, low, whole, arrived[name], dve if name in ("o", "up") else pool))
            take(lead, 8)

        m = arrived["l2"]
        dve(lambda e, i: e.scalar_tensor_tensor(out=wbase[:, :, :], in0=wbias, scalar=DELTA_SCALE,
                                                in1=wbase[:, :, :], op0=ALU.mult, op1=ALU.add), [m])
        slot["HW"].free = [dve.mark()]
        tt(dve, w2_bc[:, :], w2_bc[:, :], w2_bc[:, :], ALU.mult, [m])

        dve(lambda e, i: e.tensor_reduce(quant[:, 0, 0:1], DW[:, :], AX.X, ALU.add, apply_absolute_value=True),
            [arrived["down"]])
        m = dve.mark()
        mm(psum[:, 3, 0:1], ones[:, :], quant[:, 0, 0:1], True, True, [m, const] + bank[3].free)
        m = pe.mark()
        m = ts(dve, down_mean[:, :], psum[:, 3, 0:1], 1.0 / (D * FF), 1e-5, ALU.mult, ALU.max, [m])
        bank[3].free = [m]
        dve(lambda e, i: e.reciprocal(quant[:, 0, 1:2], down_mean[:, :]), [m])
        m = dve.mark()
        m = ts(dve, DW[:, :], DW[:, :], quant[:, 0, 1:2], ROUND, ALU.mult, ALU.add, [m])
        m = ts(dve, DW[:, :], DW[:, :], ROUND, 1.0, ALU.subtract, ALU.min, [m])
        signs_ready = ts(dve, WDN[:, :, :].rearrange("p c n -> p (c n)"), DW[:, :], -1.0, None, ALU.max, ALU.bypass, [m])
        pe.wait(signs_ready, *ready)

        prog.loop(B)
        slot["X1_ready"] = [dma(c_res, X1[:, :, :], lambda i: x[bass.ds(i, 1)].rearrange("o (t p) d -> p (o t) d", p=P),
                                slot["X1"].free)]
        load_next()
        slot["bc_ready"] = [dma(c_bc, bc[:, :, :], lambda i: rows_dram[bass.ds(i, 1), 0:3 * D]
                                .rearrange("o (r d) -> o r d", r=3).broadcast_to([P, 3, D]), slot["bc"].free)]
        hyper_load(0)
        attn = attention()
        take(attn, LEAD)
        nn = norm_next(dve)
        weave((attn, 1, 6), (nn, 1, 6))
        run(nn)
        take(attn, HEADS - LEAD - 6)
        qk0, qk1, nv = qk_next(0, (2, 3)), qk_next(1, (6, 7)), v_next((7, 6))
        fin, hyp = attn_out((0, 1), (4, 5)), hyper_slice((7, 1, 4, 6))
        take(qk0, 1)
        take(attn, 1)
        activation(spare[:, :], zero[:, :], ACT.Silu)
        take(qk0, 1)
        take(attn, 1)
        take(fin, 1)
        take(nv, 1)
        take(qk0, 1)
        take(fin, 1)
        take(qk0, 1)
        mv = load_vec(lambda i: i, slot["vec"].free)
        act.wait(mv)
        na, nb = (norm(th, X1, slot["X1_tile"], FG, FB, (2 * th, 2 * th + 1), "G") for th in range(2))
        take(fin, 1)
        take(na, 1)
        run(qk0)
        take(fin, 1)
        take(na, 1)
        take(nb, 1)
        take(nv, 1)
        run(nv)
        take(hyp, 1)
        take(na, 2)
        take(nb, 2)
        take(na, 1)
        ffn, lead = swiglu(), maxima_lead((6, 7))
        take(nb, 2)
        take(ffn, 1)
        m = tt(pool, X1[:, :, :], X1[:, :, :], bc[:, R_ALPHA_F_B:R_ALPHA_F_B + 1, :].broadcast_to([P, TT, D]), ALU.add,
               slot["rms1"].free)
        slot["X1_ready"] = [m]
        take(ffn, 5)
        weave((ffn, 1, 4 * FC - 8), (lead, 1, 4 * FC - 8))
        activation(spare[:, :], zero[:, :], ACT.Gelu)
        na, nb = (norm(th, X1, slot["X1_tile"], L1S, None, (2 * th, 2 * th + 1)) for th in range(2))
        take(hyp, 1)
        take(ffn, 1)
        take(ffn, 1)
        take(na, 1)
        run(ffn)
        take(na, 1)
        take(nb, 1)
        take(qk1, 2)
        take(hyp, 1)
        take(na, 2)
        take(nb, 2)
        take(na, 1)
        take(nb, 2)
        l1 = geglu()
        take(qk1, 1)
        take(l1, 2)
        run(qk1)
        weave((l1, 2, 2), (lead, 2, 2))
        weave((l1, 2, 4), (lead, 1, 4))
        take(l1, 2)
        take(hyp, 1)
        take(l1, 2)
        run(lead)
        run(l1)
        slot["vec"].free = slot["vec_read"]
        for name in ("stacks0", "stacks1", "V_ready"):
            prog.section.left[name] = slot[name]
        for g in range(LEAD // G):
            prog.section.left[f"mrow{g}"] = slot["mrow"][g]
        prog.end_loop()
        big.close()

        def each(name, shape, dt=F32):
            return [sb(f"{name}{k}", shape, dt) for k in range(UNROLL)]

        x3 = each("x3_", [P, TT, D])
        xr = each("xr", [P, TT, D])
        xth, xtl = each("xth", [P, KC, T], F32R), each("xtl", [P, KC, T], F32R)
        raw = each("raw", [P, 2, D])
        wb = each("wb", [P, 2, D])
        wbh, wbl = each("wbh", [P, 2, D], F32R), each("wbl", [P, 2, D], F32R)
        dn = each("dn", [P, T])
        dnh, dnl = each("dnh", [P, T], F32R), each("dnl", [P, T], F32R)
        y = each("y", [P, TT, D])
        l3row = each("l3row", [P, D])
        stats = each("stats", [P, TT, 6])
        mv2 = each("mv", [P, TT, 2])
        rstd = each("rstd", [P, 2, TT])
        c_x3, c_raw, c_l3, c_y = ([prog.dma_counter(f"{n}_{k}") for k in range(UNROLL)] for n in ("x3", "raw", "l3", "y"))
        s2 = {f"{n}{k}": prog.slot(f"t_{n}{k}")
              for n in ("x3", "xr", "xt", "raw", "wb", "wbp", "dn", "dnp", "y", "l3", "st") for k in range(UNROLL)}

        def load_batch(k, at):
            there = {}
            there["x3"] = dma(c_x3[k], x3[k][:, :, :],
                              lambda i: mid_dram[bass.ds(at(i), 1)].rearrange("o p t d -> (o p) t d"), s2[f"x3{k}"].free)
            for kc in range(KC):
                dma(c_raw[k], raw[k][:, 0, kc * BN:(kc + 1) * BN],
                    lambda i, kc=kc: hyper_dram[bass.ds(at(i) + kc * B, 1), 0:HYPER // 2]
                    .rearrange("o (p n) -> (o p) n", p=P), s2[f"raw{k}"].free)
                there["raw"] = dma(c_raw[k], raw[k][64 * kc:64 * kc + 64, 1, :],
                                   lambda i, kc=kc: hyper_dram[bass.ds(at(i) + kc * B, 1), HYPER // 2:HYPER]
                                   .rearrange("o (p n) -> (o p) n", p=64))
            slot[f"loaded{k}"] = there

        def load_row(k, at):
            there = slot[f"loaded{k}"]
            there["l3"] = dma(c_l3[k], l3row[k][:, :],
                              lambda i: rows_dram[bass.ds(at(i), 1), 3 * D:4 * D].broadcast_to([P, D]), s2[f"l3{k}"].free)

        everything = [Mark(c, prog.sections[0], c.n) for c in prog.counters if c.n]
        for e in (pe, act, dve, pool, sp):
            e.wait(*everything)
        for k in range(UNROLL):
            load_batch(k, lambda i, k=k: k)
        for k in range(UNROLL):
            load_row(k, lambda i, k=k: k)

        prog.loop(B // UNROLL, own=c_x3 + c_raw + c_l3)
        for k in range(UNROLL):
            slot[f"loaded{k}"] = {n: f"{n}_loaded{k}" for n in ("x3", "raw", "l3")}

        def l2l3(k):
            b0 = 4 * (k % 2)
            xk, xo = x3[k], xr[k]
            loaded = slot[f"loaded{k}"]
            row_here = loaded["l3"]
            dve(lambda e, i: e.scalar_tensor_tensor(out=wb[k][:, :, :], in0=raw[k][:, :, :], scalar=DELTA_SCALE,
                                                    in1=wbase[:, :, :], op0=ALU.mult, op1=ALU.add),
                [loaded["raw"]] + s2[f"wb{k}"].free)
            m = dve.mark()
            s2[f"raw{k}"].free = [m]
            mh = activation(wbh[k][:, :, :], wb[k][:, :, :], ACT.Copy, [m] + s2[f"wbp{k}"].free)
            mp = tt(pool, xo[:, :, :], xk[:, :, :], bu_bc[:, :].unsqueeze(1).broadcast_to([P, TT, D]), ALU.add,
                    [loaded["x3"]] + s2[f"xr{k}"].free)
            x_read = []
            for c in range(KC):
                bk = b0 + c
                for t in range(TT):
                    transpose(psum[:, bk, t * P:(t + 1) * P], xk[:, t, c * P:(c + 1) * P], ident[:, :],
                              [loaded["x3"]] + bank[bk].free)
                m = pe.mark()
                mx = activation(xth[k][:, c, :], psum[:, bk, :], ACT.Copy, [m] + s2[f"xt{k}"].free)
                if c == 0:
                    w_ready = tt(dve, wbl[k][:, :, :], wb[k][:, :, :], f32(wbh[k][:, :, :]), ALU.subtract, [mh])
                    s2[f"wb{k}"].free = [w_ready]
                x_ready = tt(dve, xtl[k][:, c, :], psum[:, bk, :], f32(xth[k][:, c, :]), ALU.subtract, [mx])
                bank[bk].free = [x_ready]
            s2[f"x3{k}"].free = [m, mp]
            yield
            bk = b0 + 2
            q = 0
            for w, h in ((wbh, xth), (wbh, xtl), (wbl, xth)):
                for kc in range(KC):
                    mm(psum[:, bk, :], w[k][:, 0, kc * BN:(kc + 1) * BN], h[k][:, kc, :], q == 0, q == 5,
                       [w_ready, x_ready] + bank[bk].free)
                    q += 1
            m = pe.mark()
            s2[f"xt{k}"].free = [m]
            load_batch(k, lambda i: (UNROLL * i + k + UNROLL) % B)
            m = activation(dn[k][:, :], psum[:, bk, :], ACT.Relu, [m] + s2[f"dn{k}"].free, bias=bd_col[:, :])
            bank[bk].free = [m]
            mh = activation(dnh[k][:, :], dn[k][:, :], ACT.Copy, [m] + s2[f"dnp{k}"].free)
            ml = tt(dve, dnl[k][:, :], dn[k][:, :], f32(dnh[k][:, :]), ALU.subtract, [mh])
            s2[f"dn{k}"].free = [ml]
            yield
            for th in range(2):
                bk = b0 + (0, 3)[th]
                for t2 in range(2):
                    t = 2 * th + t2
                    q = 0
                    for h, w in ((dnh, wbh), (dnh, wbl), (dnl, wbh)):
                        mm(psum[:, bk, t2 * D:(t2 + 1) * D], h[k][:, t * P:(t + 1) * P], w[k][:, 1, :], q == 0, q == 2,
                           [ml] + bank[bk].free)
                        q += 1
                m = pe.mark()
                xt2 = xo[:, 2 * th:2 * th + 2, :]
                m2 = tt(dve, xt2, psum[:, bk, :].rearrange("p (t d) -> p t d", t=2), xt2, ALU.add, [m, mp])
                bank[bk].free = [m2]
                for t in (2 * th, 2 * th + 1):
                    dve(lambda e, i, t=t: e.bn_stats(stats[k][:, t, :], xo[:, t, :]), [m2])
            s2[f"dnp{k}"].free = [m]
            s2[f"wbp{k}"].free = [m]
            m = dve.mark()
            for t in range(TT):
                dve(lambda e, i, t=t: e.bn_aggr(mv2[k][:, t, :], stats[k][:, t, :]), [m] + s2[f"st{k}"].free, carried=True)
            m_s = dve.mark()
            m = ts(pool, rstd[k][:, 0, :], mv2[k][:, :, 1], 1.0, LN_EPS, ALU.mult, ALU.add, [m_s] + s2[f"st{k}"].free)
            m_r = tt(pool, rstd[k][:, 1, :], rstd[k][:, 0, :], mhalf[:, :], ALU.pow, [m])
            yield
            for t in range(TT):
                ts(dve, y[k][:, t, :], xo[:, t, :], mv2[k][:, t, 0:1], rstd[k][:, 1, t:t + 1], ALU.subtract, ALU.mult,
                   [m_r] + s2[f"y{k}"].free)
            m = dve.mark()
            s2[f"xr{k}"].free = [m]
            s2[f"st{k}"].free = [m]
            yield
            m = tt(dve, y[k][:, :, :], y[k][:, :, :], w2_bc[:, :].unsqueeze(1).broadcast_to([P, TT, D]), ALU.mult, [m])
            m = tt(pool, y[k][:, :, :], y[k][:, :, :], l3row[k][:, :].unsqueeze(1).broadcast_to([P, TT, D]), ALU.add,
                   [m, row_here])
            s2[f"l3{k}"].free = [m]
            m = dma(c_y[k], lambda i: out[bass.ds(UNROLL * i + k, 1)].rearrange("o (t p) d -> p (o t) d", p=P),
                    y[k][:, :, :], [m])
            s2[f"y{k}"].free = [m]
            load_row(k, lambda i: (UNROLL * i + k + UNROLL) % B)
            yield

        flows = [l2l3(n) for n in range(UNROLL)]
        for turn in range(STAGGER * (UNROLL - 1) + 5):
            for n, flow in enumerate(flows):
                if turn >= STAGGER * n:
                    next(flow, None)
        for k in range(UNROLL):
            for n, m in slot[f"loaded{k}"].items():
                prog.section.left[f"{n}_loaded{k}"] = [m]
        prog.end_loop()
        sp.wait(*[Mark(c, prog.sections[0], c.n) for c in c_y + c_x3 + c_raw + c_l3])

        block = ctx.enter_context(nc.Block())
        block.sync(sp.play)
        block.gpsimd(pool.play)
        block.scalar(act.play)
        block.vector(dve.play)
        block.tensor(pe.play)


def kernel(x, cond_256, L0_cond_attn_gamma_w, L0_cond_attn_beta_w, L0_cond_W_q, L0_cond_W_k, L0_cond_W_v, L0_cond_W_o,
           L0_cond_attn_alpha_w, L0_cond_ffn_gamma_w, L0_cond_ffn_beta_w, L0_cond_gate_w, L0_cond_hidden_w, L0_cond_out_w,
           L0_cond_out_b, L0_cond_ffn_alpha_w, L1_cond_norm_w, L1_cond_up_w, L1_cond_down_w, L2_cond_Wd, L2_cond_bd,
           L2_cond_Wu, L2_cond_bu, L2_cond_Wdd, L2_cond_bdd, L2_cond_Wdu, L2_cond_bdu, L3_cond_weight, L3_cond_bias,
           L3_cond_lin_w, L3_cond_lin_b):
    import concourse.bacc as bacc
    from concourse.bass_utils import run_bass_kernel_spmd

    def a(v):
        return np.asarray(v)

    def tr(*ws):
        return np.concatenate([a(w) for w in ws], axis=0).T

    wdd = a(L2_cond_Wdd).reshape(BN, D, NC).transpose(2, 1, 0).reshape(NC, 2, -1)
    wdu = a(L2_cond_Wdu).reshape(D, BN, NC).transpose(2, 1, 0).reshape(NC, 2, -1)
    hyper = np.concatenate([wdd, wdu], axis=2).transpose(1, 0, 2).reshape(2 * NC, -1)
    arrays = {
        "x": a(x),
        "cond_t": a(cond_256).T,
        "vec_t": tr(L0_cond_attn_gamma_w, L0_cond_attn_beta_w, L0_cond_ffn_gamma_w, L0_cond_ffn_beta_w, L1_cond_norm_w),
        "row_t": tr(L0_cond_attn_alpha_w, L0_cond_ffn_alpha_w, L3_cond_lin_w),
        "wqk_t": tr(L0_cond_W_q, L0_cond_W_k),
        "wv_t": tr(L0_cond_W_v),
        "wo_t": tr(L0_cond_W_o),
        "wg_t": tr(L0_cond_gate_w),
        "wh_t": tr(L0_cond_hidden_w),
        "wout_t": tr(L0_cond_out_w),
        "out_b": a(L0_cond_out_b),
        "wup_t": tr(L1_cond_up_w),
        "wdown_t": tr(L1_cond_down_w),
        "hyper": hyper,
        "wd_t": tr(L2_cond_Wd),
        "bdd_t": a(L2_cond_bdd).reshape(BN, D).T,
        "wu_t": tr(L2_cond_Wu),
        "bdu_t": a(L2_cond_bdu).reshape(D, BN).T,
        "bd": a(L2_cond_bd),
        "bu": a(L2_cond_bu),
        "lin_b": a(L3_cond_lin_b),
        "ln_w": a(L3_cond_weight),
        "ln_b": a(L3_cond_bias),
    }
    nc = bacc.Bacc("TRN2", target_bir_lowering=False, num_devices=1)
    ins, args = {}, []
    for name, v in arrays.items():
        v = np.ascontiguousarray(v)
        ins["in_" + name] = v
        args.append(nc.dram_tensor("in_" + name, v.shape, mybir.dt.from_np(v.dtype), kind="ExternalInput").ap())
    out = nc.dram_tensor("out", (B, T, D), F32, kind="ExternalOutput").ap()
    cond_seq(nc, *args, out)
    return run_bass_kernel_spmd(nc, [ins], core_ids=[0]).results[0]["out"]
```
